# Optimizing a Trainium2 kernel written in Bass

```python
import numpy as np
import jax
import jax.numpy as jnp

def _softmax(x, axis=-1):
    return jax.nn.softmax(x, axis=axis)

def _gelu(x):
    return jax.nn.gelu(x, approximate=True)

def _silu(x):
    return jax.nn.silu(x)

def _sigmoid(x):
    return jax.nn.sigmoid(x)

def _layernorm(x, axis=-1, eps=1e-05):
    m = jnp.mean(x, axis=axis, keepdims=True)
    v = jnp.var(x, axis=axis, keepdims=True)
    return (x - m) / jnp.sqrt(v + eps)

def _scatter_add(tgt, idx, src, axis=0):
    return tgt.at[idx].add(src)

def _segment_sum(src, seg, n):
    return jax.ops.segment_sum(src, seg, n)
kernel_name = 'mk_adaln_d1_jaxref_r4_572efa'

def setup_inputs(seed: int=0):
    np.random.seed(seed)
    _w = jnp.asarray

    def _L0_attn_setup():
        import jax, jax.numpy as jnp
        import numpy as np
        B, S, E, H = (4, 1024, 256, 16)
        D = E // H

        def _xavier(key, out_f, in_f):
            lim = float(np.sqrt(6.0 / (in_f + out_f)))
            return jax.random.uniform(key, (out_f, in_f), jnp.float32, -lim, lim)

        def _feature_map(t):
            return jax.nn.elu(t) + 1.0
        key = jax.random.key(seed)
        ks = jax.random.split(key, 9)
        x = jax.random.normal(ks[0], (B, S, E), jnp.float32)
        Wq = _xavier(ks[1], E, E)
        Wk = _xavier(ks[2], E, E)
        Wv = _xavier(ks[3], E, E)
        Wo = _xavier(ks[4], E, E)
        bq = jnp.zeros((E,), jnp.float32)
        bk = jnp.zeros((E,), jnp.float32)
        bv = jnp.zeros((E,), jnp.float32)
        bo = jnp.zeros((E,), jnp.float32)
        return {'x': x, 'Wq': Wq, 'bq': bq, 'Wk': Wk, 'bk': bk, 'Wv': Wv, 'bv': bv, 'Wo': Wo, 'bo': bo}
    _L0_attn_in = _L0_attn_setup()

    def _L0_ffn_setup():
        import jax, jax.numpy as jnp
        import numpy as np
        D_MODEL = 256
        D_FF = 1024
        N_EXPERTS = 8
        D_EXPERT = D_FF // N_EXPERTS
        TOP_K = 2
        LB_WEIGHT = 0.01
        B, S = (4, 512)

        def _top_k_softmax(logits, k):
            vals, _ = jax.lax.top_k(logits, k)
            thresh = vals[..., -1:]
            masked = jnp.where(logits >= thresh, logits, -jnp.inf)
            return jax.nn.softmax(masked, axis=-1)
        key = jax.random.key(seed)
        ks = jax.random.split(key, 8)
        x = jax.random.normal(ks[0], (B, S, D_MODEL), dtype=jnp.float32)
        w1 = jax.random.normal(ks[1], (N_EXPERTS, D_MODEL, D_EXPERT), dtype=jnp.float32) * (1.0 / np.sqrt(D_MODEL))
        b1 = jnp.zeros((N_EXPERTS, D_EXPERT), dtype=jnp.float32)
        w2 = jax.random.normal(ks[2], (N_EXPERTS, D_EXPERT, D_MODEL), dtype=jnp.float32) * (1.0 / np.sqrt(D_EXPERT))
        b2 = jnp.zeros((N_EXPERTS, D_MODEL), dtype=jnp.float32)
        centroids = jax.random.normal(ks[3], (N_EXPERTS, D_MODEL), dtype=jnp.float32) * 0.02
        w_route = jax.random.normal(ks[4], (N_EXPERTS, D_MODEL), dtype=jnp.float32) * (1.0 / np.sqrt(D_MODEL))
        return {'x': x, 'w1': w1, 'b1': b1, 'w2': w2, 'b2': b2, 'centroids': centroids, 'w_route': w_route}
    _L0_ffn_in = _L0_ffn_setup()
    _L0_c = _w((lambda *s: np.random.randn(*s).astype(np.float32) * 0.05)(2, 256))
    _L0_wmod = _w((lambda *s: np.random.randn(*s).astype(np.float32) * 0.05)(256, 6 * 256) * 256 ** (-0.5))
    _d = {'L0_attn_x': _L0_attn_in['x'], 'L0_attn_Wq': _L0_attn_in['Wq'], 'L0_attn_bq': _L0_attn_in['bq'], 'L0_attn_Wk': _L0_attn_in['Wk'], 'L0_attn_bk': _L0_attn_in['bk'], 'L0_attn_Wv': _L0_attn_in['Wv'], 'L0_attn_bv': _L0_attn_in['bv'], 'L0_attn_Wo': _L0_attn_in['Wo'], 'L0_attn_bo': _L0_attn_in['bo'], 'L0_ffn_w1': _L0_ffn_in['w1'], 'L0_ffn_b1': _L0_ffn_in['b1'], 'L0_ffn_w2': _L0_ffn_in['w2'], 'L0_ffn_b2': _L0_ffn_in['b2'], 'L0_ffn_centroids': _L0_ffn_in['centroids'], 'L0_ffn_w_route': _L0_ffn_in['w_route'], 'L0_c': _L0_c, 'L0_wmod': _L0_wmod}
    _x0 = _d['L0_attn_x']
    _d['L0_attn_x'] = jax.random.normal(jax.random.fold_in(jax.random.key(seed), 1), (2, 2048, 256), dtype=_x0.dtype)
    del _x0
    return _d

def reference(L0_attn_x, L0_attn_Wq, L0_attn_bq, L0_attn_Wk, L0_attn_bk, L0_attn_Wv, L0_attn_bv, L0_attn_Wo, L0_attn_bo, L0_ffn_w1, L0_ffn_b1, L0_ffn_w2, L0_ffn_b2, L0_ffn_centroids, L0_ffn_w_route, L0_c, L0_wmod):

    def _L0_attn_ref(x, Wq, bq, Wk, bk, Wv, bv, Wo, bo):
        import jax, jax.numpy as jnp
        import numpy as np
        B, S, E, H = (4, 1024, 256, 16)
        D = E // H

        def _xavier(key, out_f, in_f):
            lim = float(np.sqrt(6.0 / (in_f + out_f)))
            return jax.random.uniform(key, (out_f, in_f), jnp.float32, -lim, lim)

        def _feature_map(t):
            return jax.nn.elu(t) + 1.0
        b, s, _ = x.shape
        Q = (x @ Wq.T + bq).reshape(b, s, H, D)
        K = (x @ Wk.T + bk).reshape(b, s, H, D)
        V = (x @ Wv.T + bv).reshape(b, s, H, D)
        Q = _feature_map(Q)
        K = _feature_map(K)
        KV = jnp.einsum('bshd,bshe->bhde', K, V)
        K_sum = K.sum(axis=1)
        Z = 1.0 / (jnp.einsum('bshd,bhd->bsh', Q, K_sum) + 1e-06)
        out = jnp.einsum('bshd,bhde,bsh->bshe', Q, KV, Z)
        out = out.reshape(b, s, E)
        out = out @ Wo.T + bo
        return out

    def _L0_ffn_ref(x, w1, b1, w2, b2, centroids, w_route):
        import jax, jax.numpy as jnp
        import numpy as np
        D_MODEL = 256
        D_FF = 1024
        N_EXPERTS = 8
        D_EXPERT = D_FF // N_EXPERTS
        TOP_K = 2
        LB_WEIGHT = 0.01
        B, S = (4, 512)

        def _top_k_softmax(logits, k):
            vals, _ = jax.lax.top_k(logits, k)
            thresh = vals[..., -1:]
            masked = jnp.where(logits >= thresh, logits, -jnp.inf)
            return jax.nn.softmax(masked, axis=-1)
        eps = 1e-12
        x_norm = x / jnp.maximum(jnp.linalg.norm(x, axis=-1, keepdims=True), eps)
        c_norm = centroids / jnp.maximum(jnp.linalg.norm(centroids, axis=-1, keepdims=True), eps)
        cos_scores = jnp.einsum('bsd,ed->bse', x_norm, c_norm)
        route_scores = jnp.einsum('bsd,ed->bse', x, w_route)
        logits = cos_scores + route_scores
        gates = _top_k_softmax(logits, TOP_K)
        h = jax.nn.gelu(jnp.einsum('bsd,edh->bseh', x, w1) + b1, approximate=False)
        expert_out = jnp.einsum('bseh,ehd->bsed', h, w2) + b2
        out = jnp.einsum('bse,bsed->bsd', gates, expert_out)
        return out
    x = L0_attn_x
    mod = (_silu(L0_c) @ L0_wmod).reshape(L0_c.shape[0], 6, 1, -1)
    sa, ca, ga, sb, cb, gb = (mod[:, 0], mod[:, 1], mod[:, 2], mod[:, 3], mod[:, 4], mod[:, 5])
    ga = (2 * (ga >= 0) - 1) * jnp.maximum(jnp.abs(ga), 0.25)
    gb = (2 * (gb >= 0) - 1) * jnp.maximum(jnp.abs(gb), 0.25)
    h = _layernorm(x, axis=-1) * (1 + ca) + sa
    x = x + ga * _L0_attn_ref(h, L0_attn_Wq, L0_attn_bq, L0_attn_Wk, L0_attn_bk, L0_attn_Wv, L0_attn_bv, L0_attn_Wo, L0_attn_bo)
    h = _layernorm(x, axis=-1) * (1 + cb) + sb
    x = x + gb * _L0_ffn_ref(h, L0_ffn_w1, L0_ffn_b1, L0_ffn_w2, L0_ffn_b2, L0_ffn_centroids, L0_ffn_w_route)
    return x

_drawn_inputs = setup_inputs


def setup_inputs(seed=0):
    import zlib

    import numpy as np

    out = dict(_drawn_inputs(seed))
    spreads = {'L0_attn_bq': (0.0, 0.8),
     'L0_attn_bk': (0.0, 0.8),
     'L0_attn_bv': (0.0, 0.29),
     'L0_attn_bo': (0.0, 0.276),
     'L0_ffn_b1': (0.0, 0.645),
     'L0_ffn_b2': (0.0, 0.434)}
    factors = {'L0_attn_Wq': 8.0, 'L0_attn_Wk': 8.0, 'L0_attn_Wv': 5.451, 'L0_ffn_centroids': 2.667}
    for name, (base, spread) in spreads.items():
        noise = np.random.default_rng([zlib.crc32(name.encode()), seed]).standard_normal(out[name].shape)
        drawn = base * np.exp(spread * noise) if base else spread * noise
        out[name] = jnp.asarray(drawn.astype(out[name].dtype))
    for name, factor in factors.items():
        out[name] = (out[name] * factor).astype(out[name].dtype)
    return out
```

```python
import concourse.bass as bass
from concourse import mybir
from contextlib import ExitStack


F32 = mybir.dt.float32
F32R = mybir.dt.float32r
ALU = mybir.AluOpType
ACT = mybir.ActivationFunctionType
AXX = mybir.AxisListType.X

P = 128
LN_EPS = 1e-5
DEN_EPS = 1e-6
NORM_EPS2 = 1e-24
GATE_MIN = 0.25
PEEL = 2


class Unit:

    def __init__(self, it, h, n_units, per_batch):
        self.it, self.h, self.n_units, self.per_batch = it, h, n_units, per_batch

    def plus(self, d):
        k = self.h + d
        u = Unit(self.it + k // 2 if k // 2 else self.it, k % 2, self.n_units, self.per_batch)
        if isinstance(self.it, int) and not 0 <= 2 * u.it + u.h < self.n_units:
            return None
        return u

    def count(self, n=1, c=0):
        return self.it * (2 * n) + (self.h * n + c)

    def tile(self, t):
        return self.it * 4 + (2 * self.h + t)

    def batch(self):
        return self.it // (self.per_batch // 2)


def wait(eng, sem, value):
    if isinstance(value, int) and value <= 0:
        return
    eng.wait_ge(sem, value)


N_SMALL = 9


def adaln_block(nc, x, wqkvT, bqk, bvT, woT, bo, w1, b1T, w2, b2, routeT, cT, wmod, out):
    S, E = x.shape
    B = cT.shape[1]
    NE, _, HID = w1.shape
    NC = E // P
    NT = S // P
    NU = NT // 2
    UPB = NU // B
    D = 16
    NH = E // D
    assert NC == 2 and HID == P and NE == 8 and UPB % 2 == 0
    NP = NE // 2

    ctx = ExitStack()
    with ctx:
        def sb(name, shape, dt=F32):
            return ctx.enter_context(nc.sbuf_tensor(name, shape, dt))

        def sem(name):
            return ctx.enter_context(nc.semaphore(name))

        def units():
            first = [Unit(u // 2, u % 2, NU, UPB) for u in range(PEEL)]
            last = [Unit(u // 2, u % 2, NU, UPB) for u in range(NU - PEEL, NU)]
            return first, last

        def pipeline(eng, step):
            first, last = units()
            for u in first:
                step(u)
            with eng.Fori(PEEL // 2, (NU - PEEL) // 2) as it:
                for h in range(2):
                    step(Unit(it, h, NU, UPB))
            for u in last:
                step(u)

        x_sb = sb("x_sb", [P, NT, E])
        q_sb = sb("q_sb", [P, NT, E])
        ident = sb("ident", [P, P])
        ones_f = sb("ones_f", [P, P])
        ones_r = sb("ones_r", [P, P], F32R)
        head_mask = sb("head_mask", [P, P])
        sel = sb("sel", [P, NE, P], F32R)
        minus_half = sb("minus_half", [P, NE])

        c_sb = sb("c_sb", [P, NC, B])
        c_exp = sb("c_exp", [P, NC, B])
        c_den = sb("c_den", [P, NC, B])
        c_rec = sb("c_rec", [P, NC, B])
        c_silu = sb("c_silu", [P, NC, B])
        c_rep = sb("c_rep", [P, NC, B, P])
        early = sb("early", [P, NC * 6 * E])
        wmod_sb = early[:, :].rearrange("p (c n) -> p c n", c=NC)
        prod = early[:, 0:4 * E].rearrange("p (h t e) -> p h t e", h=2, t=2)
        mod_col = sb("mod_col", [P, 4, B])
        mod_row = sb("mod_row", [P, B, 4, E])

        gate_sign, gate_abs, gate_size = (q_sb[:, NT - 11 - i, :] for i in range(3))

        wm_raw = sb("wm_raw", [P, NC * 3 * E])
        wm_hi = sb("wm_hi", [P, NC * 3 * E], F32R)
        wm_lo = sb("wm_lo", [P, NC * 3 * E], F32R)
        wqkv_raw, wqkv_hi, wqkv_lo = (m[:, :].rearrange("p (c n) -> p c n", c=NC) for m in (wm_raw, wm_hi, wm_lo))
        m_f, m_hi, m_lo = (m[:, 0:B * NC * E].rearrange("p (b c n) -> p b c n", b=B, c=NC)
                           for m in (wm_raw, wm_hi, wm_lo))
        tail = q_sb[:, NT - 10:NT, :].rearrange("p t e -> p (t e)")
        bqk_raw = tail[0:33, 0:2 * E]
        bqk_t = tail[0:33, 2 * E:4 * E].bitcast(F32R)
        bo_raw = tail[0:33, 4 * E:5 * E]
        bo_g = tail[0:33, 5 * E:7 * E].rearrange("p (b e) -> p b e", b=B)
        bo_t = tail[0:33, 7 * E:9 * E].bitcast(F32R).rearrange("p (b e) -> p b e", b=B)
        b2_raw = tail[0:2 * NE, 9 * E:10 * E]
        bqk_r = sb("bqk_r", [P, 2 * E], F32R)
        bv_sb = sb("bv_sb", [P, NC])
        wo_sb = sb("wo_sb", [P, NC, E])
        bo_r = sb("bo_r", [P, B, E], F32R)
        shared = sb("shared", [P, NE * E])
        w1_raw = shared[:, :].rearrange("p (c e j) -> p c e j", c=NC, e=NE)
        w2_raw = shared[:, :].rearrange("p (e d) -> p e d", e=NE)
        hid, hid_g = (shared[:, i * 4 * E:(i + 1) * 4 * E].rearrange("p (s j n) -> p s j n", s=2, j=2) for i in range(2))
        w1_hi = sb("w1_hi", [P, NC, NE, HID], F32R)
        w1_lo = sb("w1_lo", [P, NC, NE, HID], F32R)
        b1_sb = sb("b1_sb", [P, NE])
        w2_hi = sb("w2_hi", [P, NE, E], F32R)
        w2_lo = sb("w2_lo", [P, NE, E], F32R)
        b2_hi = sb("b2_hi", [P, E], F32R)
        b2_lo = sb("b2_lo", [P, E], F32R)
        route_raw = sb("route_raw", [P, NC, 2 * NE])
        route_hi = sb("route_hi", [P, NC, 2 * NE], F32R)
        route_lo = sb("route_lo", [P, NC, 2 * NE], F32R)
        cent_sq = sb("cent_sq", [P, NC, NE])
        cent_n2 = sb("cent_n2", [P, NE])
        cent_rn = sb("cent_rn", [P, NE])

        stats = sb("stats", [P, 2, 2, 6])
        mv = sb("mv", [P, 2, 2, 2])
        var_eps = sb("var_eps", [P, 2, 2])
        neg_mean = sb("neg_mean", [P, 2, 2])
        rstd = sb("rstd", [P, 2, 2])
        neg_mr = sb("neg_mr", [P, 2, 2])
        nat = sb("nat", [P, 2, 2, E])
        tr_f = sb("tr_f", [P, 2, NC, 2 * P])
        tr_hi = sb("tr_hi", [P, 2, NC, 2 * P], F32R)
        tr_lo = sb("tr_lo", [P, 2, NC, 2 * P], F32R)
        e_sb = sb("e_sb", [P, 2, 2 * E])
        sel_f = e_sb[:, :, :].rearrange("p t (e q) -> p (t e) q", q=P)
        k_sb = sb("k_sb", [P, 2, 2, E])
        xc, y_g = k_sb[:, 0, :, :], k_sb[:, 1, :, :]
        v_sb = sb("v_sb", [P, 2, 2, E])
        sq = v_sb[:, 0, 0, :]
        lg_t = v_sb[0:2 * NE, 1, 0, :]
        k_sum = sb("k_sum", [P, B, E])
        kv_acc = sb("kv_acc", [P, B, NC, P])
        ksum_row = sb("ksum_row", [P, B, E])
        kv_b = tr_f[:, 0, 0, :].rearrange("p (c n) -> p c n", c=NC)
        kv_m = tr_f[:, 1, :, :].rearrange("p b (c n) -> p b c n", c=NC)
        den = sb("den", [P, 2, 2, NH])
        den_e = sb("den_e", [P, 2, 2, NH])
        z = sb("z", [P, 2, 2, NH])
        h_n2 = sb("h_n2", [P, 2, 2])
        h_n2c = sb("h_n2c", [P, 2, 2])
        h_rn = sb("h_rn", [P, 2, 2])
        cosw = sb("cosw", [P, 2, NE])
        logit = sb("logit", [P, 2, NE])
        top = sb("top", [P, 2, 8])
        shifted = sb("shifted", [P, 2, NE])
        chosen = sb("chosen", [P, 2, NE])
        g_exp = sb("g_exp", [P, 2, NE])
        g_sel = sb("g_sel", [P, 2, NE])
        g_sum = sb("g_sum", [P, 2])
        g_rec = sb("g_rec", [P, 2])
        g_f = sb("g_f", [P, 2, NE])
        g_hir = sb("g_hir", [P, 2, NE], F32R)
        g_hilo = sb("g_hilo", [P, 2, 2 * NE])
        gT = sb("gT", [P, 2, 2 * P], F32R)
        hid_hi = sb("hid_hi", [P, 2, 2, 2 * P], F32R)
        hid_lo = sb("hid_lo", [P, 2, 2, 2 * P], F32R)

        bank = [ctx.enter_context(nc.psum_tensor(f"bank{i}", [P, 512], F32)) for i in range(8)]
        chunks = "p (c n) -> p c n"

        d_c = sem("d_c"); d_wmod = sem("d_wmod"); d_qkv = sem("d_qkv"); d_wo = sem("d_wo")
        d_w1 = sem("d_w1"); d_w2 = sem("d_w2"); d_small = sem("d_small")
        x_in = [sem(f"x_in{h}") for h in range(2)]
        y_out = [sem(f"y_out{h}") for h in range(2)]
        const_step = sem("const_step"); const_ready = sem("const_ready")
        c_exp_ready = sem("c_exp_ready"); silu_step = sem("silu_step"); c_rep_ready = sem("c_rep_ready")
        modcol_done = sem("modcol_done"); modcol_ready = sem("modcol_ready")
        modrow_done = sem("modrow_done"); modrow_step = sem("modrow_step")
        qkv_step = sem("qkv_step"); qkv_ready = sem("qkv_ready")
        zero_rows = sem("zero_rows"); cent_done = sem("cent_done"); cent_n2_ready = sem("cent_n2_ready")
        cent_ready = sem("cent_ready")
        w1_step = sem("w1_step"); w1_ready = sem("w1_ready")
        w2_step = sem("w2_step"); w2_ready = sem("w2_ready"); small_step = sem("small_step")
        small_ready = sem("small_ready")

        a_st = sem("a_st"); a_stats = sem("a_stats"); a_pow = sem("a_pow"); a_rstd = sem("a_rstd")
        a_xn = sem("a_xn"); a_tp = sem("a_tp"); a_hf = sem("a_hf"); a_hi = sem("a_hi"); a_lo = sem("a_lo")
        a_qk = sem("a_qk"); a_v = sem("a_v"); a_exp = sem("a_exp"); a_vs = sem("a_vs"); a_neg = sem("a_neg")
        a_fm = sem("a_fm"); a_ks = sem("a_ks"); a_kst = sem("a_kst"); a_kv = sem("a_kv"); a_acc = sem("a_acc")
        acc_zero = sem("acc_zero")

        f_ksum = sem("f_ksum"); f_ksrow = sem("f_ksrow"); f_step = sem("f_step"); f_kvm = sem("f_kvm")
        f_m = sem("f_m"); f_ready = sem("f_ready")

        o_prod = sem("o_prod"); o_den = sem("o_den"); o_z = sem("o_z"); o_qz = sem("o_qz"); o_tp = sem("o_tp")
        o_hi = sem("o_hi"); o_lo = sem("o_lo"); o_y = sem("o_y"); o_x1 = sem("o_x1")

        e_st = sem("e_st"); e_stats = sem("e_stats"); e_rstd = sem("e_rstd"); e_xc = sem("e_xc")
        e_h = sem("e_h"); e_sq = sem("e_sq"); e_n2 = sem("e_n2"); e_rn = sem("e_rn")
        e_tp = sem("e_tp"); e_hi = sem("e_hi"); e_lo = sem("e_lo")
        e_route = sem("e_route"); e_lgs = sem("e_lgs"); e_lgT = sem("e_lgT"); e_gstep = sem("e_gstep")
        e_shift = sem("e_shift"); e_gexp = sem("e_gexp"); e_gnat = sem("e_gnat"); e_gTp = sem("e_gTp")
        e_gT = sem("e_gT")
        e_f1 = sem("e_f1"); e_gb = sem("e_gb"); e_gelu = sem("e_gelu"); e_mul = sem("e_mul")
        e_hhi = sem("e_hhi"); e_hlo = sem("e_hlo"); e_f2 = sem("e_f2"); e_yg = sem("e_yg"); e_y = sem("e_y"); e_gfs = sem("e_gfs")

        met_v = sem("met_v"); met_g = sem("met_g"); met_t = sem("met_t")

        def wait_alone(eng, met, on, value):
            wait(eng, on, value)
            if not isinstance(value, int):
                eng.sem_inc(met, 1)

        block = ctx.enter_context(nc.Block())

        @block.sync
        def _(sp):
            def load_x(it, h):
                t = it * 4 + 2 * h
                wait(sp, x_in[h], it * 16)
                sp.dma_start(x_sb[:, bass.ds(t, 2), :], x_tiles[:, bass.ds(t, 2), :]).then_inc(x_in[h], 16)

            x_tiles = x.rearrange("(t p) e -> p t e", p=P)
            out_tiles = out.rearrange("(t p) e -> p t e", p=P)
            load_x(0, 0)
            sp.dma_start(wqkv_raw[:, :, :], wqkvT.rearrange("(c p) n -> p c n", p=P)).then_inc(d_qkv, 16)
            load_x(0, 1)
            with sp.Fori(1, NU // 2) as it:
                for h in range(2):
                    load_x(it, h)
            sp.dma_start(w1_raw[:, 0, :, :], w1[:, 0:P, :].rearrange("e p j -> p e j")).then_inc(d_w1, 16)
            sp.dma_start(w1_raw[:, 1, :, :], w1[:, P:2 * P, :].rearrange("e p j -> p e j")).then_inc(d_w1, 16)
            sp.wait_ge(w1_ready, 1)
            sp.dma_start(w2_raw[:, :, :], w2.rearrange("e p d -> p e d")).then_inc(d_w2, 16)

            def store(u):
                wait(sp, e_y, u.count(1, 1))
                sp.dma_start(out_tiles[:, bass.ds(u.tile(0), 2), :],
                             x_sb[:, bass.ds(u.tile(0), 2), :]).then_inc(y_out[u.h], 16)

            pipeline(sp, store)
            for h in range(2):
                sp.wait_ge(y_out[h], 16 * (NU // 2))

        @block.gpsimd
        def _(pool):
            gp = nc.gpsimd
            gp.memset(ident[:, :], 0.0).then_inc(const_step, 1)
            gp.memset(sel_f[:, :, :], 0.0).then_inc(const_step, 1)
            gp.memset(head_mask[:, :], 1.0).then_inc(const_step, 1)
            gp.memset(minus_half[:, :], -0.5)
            gp.memset(ones_f[:, :], 1.0)
            pool.wait_ge(const_step, 3)
            gp.affine_select(out=ident[:, :], in_=ident[:, :], compare_op=ALU.not_equal, fill=1.0,
                             base=0, pattern=[[-1, P]], channel_multiplier=1)
            gp.affine_select(out=sel_f[:, :, :], in_=sel_f[:, :, :], compare_op=ALU.not_equal, fill=1.0,
                             base=0, pattern=[[-1, NE], [0, P]], channel_multiplier=1).then_inc(const_step, 1)
            heads = head_mask[:, :].rearrange("p (h d) -> p h d", d=D)
            gp.affine_select(out=heads, in_=heads, compare_op=ALU.is_ge, fill=0.0,
                             base=0, pattern=[[-D, P // D], [0, D]], channel_multiplier=1).then_inc(const_step, 1)
            pool.wait_ge(const_step, 5)
            gp.affine_select(out=sel_f[:, :, :], in_=sel_f[:, :, :], compare_op=ALU.not_equal, fill=1.0,
                             base=-NE, pattern=[[-1, NE], [0, P]], channel_multiplier=1)
            gp.affine_select(out=heads, in_=heads, compare_op=ALU.is_ge, fill=0.0,
                             base=D - 1, pattern=[[D, P // D], [0, D]], channel_multiplier=-1)\
              .then_inc(const_ready, 1)
            gp.memset(k_sum[:, :, :], 0.0).then_inc(a_kst, 1)

            def rstd_a(u):
                h = u.h
                wait(pool, a_stats, u.count(1, 1))
                wait(pool, a_xn, u.count(1, -1))
                gp.tensor_tensor(rstd[:, h, :], var_eps[:, h, :], minus_half[:, 0:2], ALU.pow).then_inc(a_pow, 1)
                wait(pool, a_pow, u.count(1, 1))
                gp.tensor_tensor(neg_mr[:, h, :], neg_mean[:, h, :], rstd[:, h, :], ALU.mult).then_inc(a_rstd, 1)

            def split_lo(u):
                h = u.h
                wait(pool, a_hi, u.count(1, 1))
                wait(pool, a_v, u.count(1, -1))
                gp.tensor_tensor(tr_lo[:, h, :, :], tr_f[:, h, :, :], tr_hi[:, h, :, :].bitcast(F32), ALU.subtract)\
                  .then_inc(a_lo, 1)

            def add_ksum(u):
                b = u.batch()
                for t in range(2):
                    wait(pool, a_fm, u.count(2, t + 1))
                    wait_alone(pool, met_g, a_kst, u.count(2, t + 1))
                    add = gp.tensor_tensor(k_sum[:, b, :], k_sum[:, b, :], k_sb[:, u.h, t, :], ALU.add)
                    add.then_inc(a_kst, 1)

            def step_a(u):
                if u.plus(1):
                    split_lo(u.plus(1))
                if u.plus(2):
                    rstd_a(u.plus(2))
                if u.plus(-1):
                    add_ksum(u.plus(-1))

            u0 = Unit(0, 0, NU, UPB)
            rstd_a(u0)
            rstd_a(u0.plus(1))
            split_lo(u0)
            pipeline(gp, step_a)
            add_ksum(Unit(NU // 2 - 1, 1, NU, UPB))

            pool.wait_ge(cent_n2_ready, 1)
            gp.tensor_tensor(cent_rn[:, :], cent_n2[:, :], minus_half[:, :], ALU.pow).then_inc(cent_ready, 1)

            def make_prod(u):
                pool.wait_ge(f_ksrow, B)
                wait_alone(pool, met_g, o_z, u.count(1, -1))
                gp.tensor_tensor(prod[:, u.h, :, :], q_sb[:, bass.ds(u.tile(0), 2), :],
                                 ksum_row[:, bass.ds(u.batch(), 1), :].to_broadcast([P, 2, E]),
                                 ALU.mult).then_inc(o_prod, 1)

            def make_qz(u):
                wait(pool, o_z, u.count(1, 1))
                wait_alone(pool, met_g, o_tp, u.count(1, -1))
                q4 = q_sb[:, bass.ds(u.tile(0), 2), :].rearrange("p t (h d) -> p (t h) d", d=D)
                n4 = nat[:, u.h, :, :].rearrange("p t (h d) -> p (t h) d", d=D)
                z4 = z[:, u.h, :, :].rearrange("p t (h o) -> p (t h) o", o=1).to_broadcast([P, 2 * NH, D])
                gp.tensor_tensor(n4, q4, z4, ALU.mult).then_inc(o_qz, 1)

            def step_o(u):
                if u.plus(2):
                    make_prod(u.plus(2))
                if u.plus(1):
                    make_qz(u.plus(1))

            make_prod(u0)
            make_prod(u0.plus(1))
            make_qz(u0)
            pipeline(gp, step_o)

            def rstd_e(u):
                wait(pool, e_stats, u.count(1, 1))
                wait(pool, e_h, u.count(1, -1))
                gp.tensor_tensor(rstd[:, u.h, :], var_eps[:, u.h, :], minus_half[:, 0:2], ALU.pow)\
                  .then_inc(e_rstd, 1)

            def norm_e(u):
                wait(pool, e_n2, u.count(1, 1))
                wait(pool, e_gnat, u.count(1, -1))
                gp.tensor_tensor(h_rn[:, u.h, :], h_n2c[:, u.h, :], minus_half[:, 0:2], ALU.pow)\
                  .then_inc(e_rn, 1)

            def lo_e(u, p):
                s = p % 2
                wait(pool, e_hhi, u.count(NP, p + 1))
                wait(pool, e_f2, u.count(NP, p - 1))
                gp.tensor_tensor(hid_lo[:, s, :, :], hid_g[:, s, :, :], hid_hi[:, s, :, :].bitcast(F32),
                                 ALU.subtract).then_inc(e_hlo, 1)

            def add_experts(u):
                wait_alone(pool, met_g, e_yg, u.count(1, 1))
                xt = x_sb[:, bass.ds(u.tile(0), 2), :]
                gp.tensor_tensor(xt, xt, y_g[:, :, :], ALU.add).then_inc(e_y, 1)

            def step_e(u):
                lo_e(u, 0)
                if u.plus(-1):
                    add_experts(u.plus(-1))
                lo_e(u, 1)
                if u.plus(1):
                    norm_e(u.plus(1))
                lo_e(u, 2)
                if u.plus(2):
                    rstd_e(u.plus(2))
                lo_e(u, 3)

            rstd_e(u0)
            norm_e(u0)
            rstd_e(u0.plus(1))
            pipeline(gp, step_e)
            add_experts(Unit(NU // 2 - 1, 1, NU, UPB))

        @block.scalar
        def _(act):
            ac = nc.scalar
            act.dma_start(c_sb[:, :, :], cT.rearrange("(c p) b -> p c b", p=P)).then_inc(d_c, 16)
            act.dma_start(wmod_sb[:, :, :], wmod.rearrange("(c p) n -> p c n", p=P)).then_inc(d_wmod, 16)
            small = [(bqk_raw[0:1, :], bqk), (bqk_raw[32:33, :], bqk), (bo_raw[0:1, :], bo), (bo_raw[32:33, :], bo),
                     (bv_sb[:, :], bvT), (b1_sb[:, :], b1T), (b2_raw[0:NE, :], b2), (b2_raw[NE:2 * NE, :], b2),
                     (route_raw[:, :, :], routeT.rearrange("(c p) n -> p c n", p=P))]
            assert len(small) == N_SMALL
            for to, of in small:
                act.dma_start(to, of).then_inc(d_small, 16)
            act.dma_start(wo_sb[:, :, :], woT.rearrange("(c p) n -> p c n", p=P)).then_inc(d_wo, 16)

            act.wait_ge(d_c, 16)
            ac.activation(c_exp[:, :, :], c_sb[:, :, :], ACT.Exp, scale=-1.0).then_inc(c_exp_ready, 1)

            def normalise(u):
                wait(act, a_rstd, u.count(1, 1))
                wait(act, a_tp, u.count(1, -1))
                for t in range(2):
                    last = ac.activation(nat[:, u.h, t, :], x_sb[:, u.tile(t), :], ACT.Identity,
                                         bias=neg_mr[:, u.h, t:t + 1], scale=rstd[:, u.h, t:t + 1])
                last.then_inc(a_xn, 1)

            def modulate(u, b):
                wait(act, a_tp, u.count(1, 1))
                wait(act, a_lo, u.count(1, -1))
                tp = bank[u.h][:, :].rearrange(chunks, c=NC)
                for c in range(NC):
                    last = ac.activation(tr_f[:, u.h, c, :], tp[:, c, :], ACT.Identity,
                                         bias=mod_col[:, c, b:b + 1] if isinstance(b, int) else mod_col[:, c, bass.ds(b, 1)],
                                         scale=mod_col[:, 2 + c, b:b + 1] if isinstance(b, int) else mod_col[:, 2 + c, bass.ds(b, 1)])
                last.then_inc(a_hf, 1)

            def negative_part(u, t):
                wait(act, a_qk, u.count(2, t + 1))
                ac.activation(e_sb[:, t, :], bank[2 + t][:, :], ACT.Relu, scale=-1.0).then_inc(a_neg, 1)

            def exp_qk(u, t):
                wait(act, a_neg, u.count(2, t + 1))
                ac.activation(e_sb[:, t, :], e_sb[:, t, :], ACT.Exp, scale=-1.0).then_inc(a_exp, 1)

            def keep_v(u):
                wait(act, a_v, u.count(1, 1))
                wait(act, a_kv, u.count(1, -1))
                ac.activation(v_sb[:, u.h, :, :].rearrange("p t e -> p (t e)"), bank[4 + u.h][:, :], ACT.Copy)\
                  .then_inc(a_vs, 1)

            def step_a(u):
                if u.plus(1):
                    modulate(u.plus(1), u.plus(1).batch())
                negative_part(u, 0)
                if u.plus(2):
                    normalise(u.plus(2))
                exp_qk(u, 0)
                negative_part(u, 1)
                exp_qk(u, 1)
                keep_v(u)

            u0 = Unit(0, 0, NU, UPB)
            normalise(u0)
            act.wait_ge(modcol_ready, 1)
            modulate(u0, 0)
            normalise(u0.plus(1))
            pipeline(ac, step_a)

            def hi_o(u):
                wait(act, o_tp, u.count(1, 1))
                wait(act, o_y, u.count(1, -1))
                ac.activation(tr_hi[:, u.h, :, :].rearrange("p c n -> p (c n)"), bank[u.h][:, :], ACT.Copy)\
                  .then_inc(o_hi, 1)

            pipeline(ac, hi_o)

            def square(u):
                wait(act, e_h, u.count(1, 1))
                wait(act, e_n2, u.count(1, -1))
                for t in range(2):
                    wait(act, e_sq, u.count(2, t))
                    ac.activation(sq[:, :], nat[:, u.h, t, :], ACT.Square,
                                  accum_out=h_n2[:, u.h, t:t + 1]).then_inc(e_sq, 1)

            def hi_e(u):
                wait(act, e_tp, u.count(1, 1))
                wait(act, e_f1, u.count(NP, -NP))
                ac.activation(tr_hi[:, u.h, :, :].rearrange("p c n -> p (c n)"), bank[0][:, :], ACT.Copy)\
                  .then_inc(e_hi, 1)

            def keep_logits(u):
                wait(act, e_route, u.count(1, 1))
                ac.activation(lg_t[:, :], bank[1][0:2 * NE, 0:2 * P], ACT.Copy).then_inc(e_lgs, 1)

            def exp_gates(u):
                wait(act, e_shift, u.count(1, 1))
                ac.activation(g_exp[:, :, :], shifted[:, :, :], ACT.Exp).then_inc(e_gexp, 1)

            def gelu(u, p):
                s = p % 2
                wait(act, e_f1, u.count(NP, p + 1))
                wait(act, e_mul, u.count(NP, p - 1))
                for j in range(2):
                    e = 2 * p + j
                    last = ac.activation(hid[:, s, j, :], bank[2 + s][:, 2 * P * j:2 * P * (j + 1)], ACT.Gelu,
                                         bias=b1_sb[:, e:e + 1])
                last.then_inc(e_gelu, 1)

            def hi_hid(u, p):
                s = p % 2
                wait(act, e_mul, u.count(NP, p + 1))
                wait(act, e_f2, u.count(NP, p - 1))
                ac.activation(hid_hi[:, s, :, :].rearrange("p j n -> p (j n)"),
                              hid_g[:, s, :, :].rearrange("p j n -> p (j n)"), ACT.Copy).then_inc(e_hhi, 1)

            def step_e(u):
                n = u.plus(1)
                gelu(u, 0)
                hi_hid(u, 0)
                if n:
                    square(n)
                gelu(u, 1)
                hi_hid(u, 1)
                if n:
                    hi_e(n)
                gelu(u, 2)
                hi_hid(u, 2)
                if n:
                    keep_logits(n)
                gelu(u, 3)
                hi_hid(u, 3)
                if n:
                    exp_gates(n)

            square(u0)
            hi_e(u0)
            keep_logits(u0)
            exp_gates(u0)
            pipeline(ac, step_e)

        @block.tensor
        def _(pe):
            te = nc.tensor

            def mm3(out_ap, l_hi, l_lo, r_hi, r_lo, start, stop):
                te.matmul(out_ap, l_hi, r_hi, start=start, stop=False)
                te.matmul(out_ap, l_hi, r_lo, start=False, stop=False)
                return te.matmul(out_ap, l_lo, r_hi, start=False, stop=stop)

            def transposes(u, to):
                dst = to[:, :].rearrange(chunks, c=NC)
                for c in range(NC):
                    for t in range(2):
                        last = te.transpose(dst[:, c, t * P:(t + 1) * P], nat[:, u.h, t, c * P:(c + 1) * P],
                                            ident[:, :])
                return last

            pe.wait_ge(d_wmod, 16)
            pe.wait_ge(c_rep_ready, 1)
            for k in range(4):
                for c in range(NC):
                    last = te.matmul(bank[7][:, k * B:(k + 1) * B], wmod_sb[:, c, k * P:(k + 1) * P],
                                     c_silu[:, c, :], start=(c == 0), stop=(c == NC - 1))
            last.then_inc(modcol_done, 1)
            for b in range(B):
                for k in range(2):
                    for c in range(NC):
                        last = te.matmul(bank[2 + 2 * b + k][:, :], c_rep[:, c, b, :],
                                         wmod_sb[:, c, 2 * E + 512 * k:2 * E + 512 * (k + 1)],
                                         start=(c == 0), stop=(c == NC - 1))
            last.then_inc(modrow_done, 1)

            def tp_a(u):
                wait(pe, a_xn, u.count(1, 1))
                wait(pe, a_hf, u.count(1, -1))
                transposes(u, bank[u.h]).then_inc(a_tp, 1)

            def qkv(u):
                h = u.h
                wait(pe, a_lo, u.count(1, 1))
                for t in range(2):
                    tok = slice(t * P, (t + 1) * P)
                    wait(pe, a_fm, u.count(2, t - 1))
                    te.matmul(bank[2 + t][:, :], ones_r[:, :], bqk_r[:, :], start=True, stop=False)
                    for c in range(NC):
                        last = mm3(bank[2 + t][:, :], tr_hi[:, h, c, tok], tr_lo[:, h, c, tok],
                                   wqkv_hi[:, c, 0:2 * E], wqkv_lo[:, c, 0:2 * E], False, c == NC - 1)
                    last.then_inc(a_qk, 1)
                wait(pe, a_vs, u.count(1, -1))
                for t in range(2):
                    tok = slice(t * P, (t + 1) * P)
                    for c in range(NC):
                        last = mm3(bank[4 + h][:, t * E:(t + 1) * E], tr_hi[:, h, c, tok], tr_lo[:, h, c, tok],
                                   wqkv_hi[:, c, 2 * E:3 * E], wqkv_lo[:, c, 2 * E:3 * E], c == 0, c == NC - 1)
                last.then_inc(a_v, 1)

            def kv(u):
                h = u.h
                wait(pe, a_fm, u.count(2, 2))
                wait(pe, a_vs, u.count(1, 1))
                wait(pe, a_acc, u.count(1, -1))
                for c in range(NC):
                    f = slice(c * P, (c + 1) * P)
                    for t in range(2):
                        last = te.matmul(bank[6 + h][:, f], v_sb[:, h, t, f], k_sb[:, h, t, f],
                                         start=(t == 0), stop=(t == 1))
                last.then_inc(a_kv, 1)

            def step_a(u):
                if u.plus(1):
                    tp_a(u.plus(1))
                qkv(u)
                if u.plus(-1):
                    kv(u.plus(-1))

            u0 = Unit(0, 0, NU, UPB)
            pe.wait_ge(const_ready, 1)
            tp_a(u0)
            pe.wait_ge(qkv_ready, 1)
            pe.wait_ge(small_ready, 1)
            pe.wait_ge(modrow_step, 8 * B)
            pipeline(te, step_a)
            kv(Unit(NU // 2 - 1, 1, NU, UPB))

            pe.wait_ge(a_acc, NU)
            for c in range(NC):
                last = te.matmul(bank[6][:, 0:NE], ones_f[:, :], cent_sq[:, c, :], start=(c == 0), stop=(c == NC - 1))
            last.then_inc(cent_done, 1)
            pe.wait_ge(a_kst, 2 * NU + 1)
            for b in range(B):
                last = te.matmul(bank[7][:, b * E:(b + 1) * E], ones_f[:, :], k_sum[:, b, :], start=True, stop=True)
            last.then_inc(f_ksum, 1)
            pe.wait_ge(d_wo, 16)
            for b in range(B):
                pe.wait_ge(f_kvm, b + 1)
                for c in range(NC):
                    last = te.matmul(bank[4 + b][:, c * E:(c + 1) * E], kv_m[:, b, c, :], wo_sb[:, c, :],
                                     start=True, stop=True)
                last.then_inc(f_m, 1)

            def tp_o(u):
                wait(pe, o_qz, u.count(1, 1))
                wait(pe, o_lo, u.count(1, -1))
                transposes(u, bank[u.h]).then_inc(o_tp, 1)

            def attend(u):
                h = u.h
                b = u.batch()
                wait(pe, o_lo, u.count(1, 1))
                wait(pe, o_x1, u.count(1, -1))
                for t in range(2):
                    tok = slice(t * P, (t + 1) * P)
                    to = bank[2 + h][:, t * E:(t + 1) * E]
                    te.matmul(to, ones_r[:, :], bo_r[:, b, :], start=True, stop=False)
                    for c in range(NC):
                        last = mm3(to, tr_hi[:, h, c, tok], tr_lo[:, h, c, tok], m_hi[:, b, c, :], m_lo[:, b, c, :],
                                   False, c == NC - 1)
                last.then_inc(o_y, 1)

            def step_o(u):
                tp_o(u)
                if u.plus(-1):
                    attend(u.plus(-1))

            pe.wait_ge(f_ready, B)
            pipeline(te, step_o)
            attend(Unit(NU // 2 - 1, 1, NU, UPB))

            def tp_e(u):
                wait(pe, e_h, u.count(1, 1))
                wait(pe, e_lo, u.count(1, 0))
                transposes(u, bank[0]).then_inc(e_tp, 1)

            def route(u):
                h = u.h
                wait(pe, e_lo, u.count(1, 1))
                wait(pe, e_gT, u.count(1, 0))
                for c in range(NC):
                    last = mm3(bank[1][0:2 * NE, 0:2 * P], route_hi[:, c, :], route_lo[:, c, :],
                               tr_hi[:, h, c, :], tr_lo[:, h, c, :], c == 0, c == NC - 1)
                last.then_inc(e_route, 1)

            def tp_logits(u):
                wait_alone(pe, met_t, e_lgs, u.count(1, 1))
                for t in range(2):
                    last = te.transpose(bank[1][:, t * 2 * NE:(t + 1) * 2 * NE], lg_t[:, t * P:(t + 1) * P],
                                        ident[0:2 * NE, 0:2 * NE])
                last.then_inc(e_lgT, 1)

            def tp_gates(u):
                wait(pe, e_gnat, u.count(1, 1))
                for t in range(2):
                    last = te.transpose(bank[1][0:2 * NE, t * P:(t + 1) * P], g_hilo[:, t, :], ident[:, :])
                last.then_inc(e_gTp, 1)

            def first(u, p):
                h, s = u.h, p % 2
                wait(pe, e_gelu, u.count(NP, p - 1))
                for j in range(2):
                    e = 2 * p + j
                    to = bank[2 + s][:, 2 * P * j:2 * P * (j + 1)]
                    for c in range(NC):
                        last = mm3(to, w1_hi[:, c, e, :], w1_lo[:, c, e, :], tr_hi[:, h, c, :], tr_lo[:, h, c, :],
                                   c == 0, c == NC - 1)
                last.then_inc(e_f1, 1)

            def spread_gates(u, p):
                s = p % 2
                if p == 0:
                    wait(pe, e_gT, u.count(1, 1))
                wait(pe, e_mul, u.count(NP, p - 1))
                for j in range(2):
                    last = te.matmul(bank[4 + s][:, 2 * P * j:2 * P * (j + 1)], sel[:, 2 * p + j, :], gT[:, u.h, :],
                                     start=True, stop=True)
                last.then_inc(e_gb, 1)

            def second(u, p):
                s = p % 2
                wait(pe, e_hlo, u.count(NP, p + 1))
                if p == 0:
                    wait(pe, e_yg, u.count(1, 0))
                for t in range(2):
                    tok = slice(t * P, (t + 1) * P)
                    to = bank[6 + t][:, 0:E]
                    if p == 0:
                        te.matmul(to, gT[:, u.h, tok], b2_hi[:, :], start=True, stop=False)
                        te.matmul(to, gT[:, u.h, tok], b2_lo[:, :], start=False, stop=False)
                    for j in range(2):
                        e = 2 * p + j
                        last = mm3(to, hid_hi[:, s, j, tok], hid_lo[:, s, j, tok], w2_hi[:, e, :],
                                   w2_lo[:, e, :], False, p == NP - 1 and j == 1)
                last.then_inc(e_f2, 1)

            def step_e(u):
                n = u.plus(1)
                first(u, 0)
                tp_gates(u)
                spread_gates(u, 0)
                if u.plus(-1):
                    second(u.plus(-1), 3)
                first(u, 1)
                spread_gates(u, 1)
                second(u, 0)
                if n:
                    tp_e(n)
                first(u, 2)
                spread_gates(u, 2)
                second(u, 1)
                if n:
                    route(n)
                first(u, 3)
                spread_gates(u, 3)
                if n:
                    tp_logits(n)
                second(u, 2)

            pe.wait_ge(o_x1, NU)
            pe.wait_ge(w1_ready, 1)
            pe.wait_ge(w2_ready, 1)
            tp_e(u0)
            route(u0)
            tp_logits(u0)
            pipeline(te, step_e)
            second(Unit(NU // 2 - 1, 1, NU, UPB), 3)

        @block.vector
        def _(dve):
            ve = nc.vector
            TT = ve.tensor_tensor

            for rows in (bqk_r[:, :], bo_r[:, :, :], b2_hi[:, :], b2_lo[:, :], gT[:, :, :]):
                last = ve.memset(rows.bitcast(F32), 0.0)
            last.then_inc(zero_rows, 1)
            ve.memset(ones_r[:, :].bitcast(F32), 1.0)
            ve.memset(kv_acc[:, :, :, :], 0.0).then_inc(acc_zero, 1)

            dve.wait_ge(c_exp_ready, 1)
            ve.tensor_scalar(c_den[:, :, :], c_exp[:, :, :], 1.0, None, ALU.add).then_inc(silu_step, 1)
            dve.wait_ge(silu_step, 1)
            ve.reciprocal(c_rec[:, :, :], c_den[:, :, :]).then_inc(silu_step, 1)
            dve.wait_ge(silu_step, 2)
            TT(c_silu[:, :, :], c_sb[:, :, :], c_rec[:, :, :], ALU.mult).then_inc(silu_step, 1)
            dve.wait_ge(silu_step, 3)
            for c in range(NC):
                last = ve.tensor_copy(c_rep[:, c, :, :],
                                      c_silu[:, c, :].rearrange("p (b o) -> p b o", o=1).to_broadcast([P, B, P]))
            last.then_inc(c_rep_ready, 1)

            def stats_of(u, x_ready, st, done, pooled):
                h = u.h
                x_ready()
                for t in range(2):
                    last = ve.bn_stats(stats[:, h, t, :], x_sb[:, u.tile(t), :])
                last.then_inc(st, 1)
                wait(dve, pooled, u.count(1, -1))
                wait_alone(dve, met_v, st, u.count(2, 1))
                for t in range(2):
                    last = ve.bn_aggr(mv[:, h, t, :], stats[:, h, t, :])
                last.then_inc(st, 1)
                wait(dve, st, u.count(2, 2))
                ve.tensor_scalar(neg_mean[:, h, :], mv[:, h, :, 0], -1.0, None, ALU.mult)
                ve.tensor_scalar(var_eps[:, h, :], mv[:, h, :, 1], LN_EPS, None, ALU.add).then_inc(done, 1)

            def stats_a(u):
                stats_of(u, lambda: dve.wait_ge(x_in[u.h], (u.it + 1) * 16), a_st, a_stats, a_rstd)

            u0 = Unit(0, 0, NU, UPB)
            stats_a(u0)
            stats_a(u0.plus(1))

            dve.wait_ge(d_qkv, 16)
            for c in range(NC):
                ve.tensor_copy(wqkv_hi[:, c, :], wqkv_raw[:, c, :]).then_inc(qkv_step, 1)
            for c in range(NC):
                dve.wait_ge(qkv_step, c + 1)
                last = TT(wqkv_lo[:, c, :], wqkv_raw[:, c, :], wqkv_hi[:, c, :].bitcast(F32), ALU.subtract)
            last.then_inc(qkv_ready, 1)

            dve.wait_ge(modcol_done, 1)
            mc = bank[7][:, 0:4 * B].rearrange("p (k b) -> p k b", b=B)
            ve.tensor_copy(mod_col[:, 0:2, :], mc[:, 0:2, :])
            ve.tensor_scalar(mod_col[:, 2:4, :], mc[:, 2:4, :], 1.0, None, ALU.add).then_inc(modcol_ready, 1)

            dve.wait_ge(modrow_done, 1)
            for b in range(B):
                first_half = bank[2 + 2 * b][:, :].rearrange("p (k e) -> p k e", k=2)
                second_half = bank[3 + 2 * b][:, :].rearrange("p (k e) -> p k e", k=2)
                ve.tensor_copy(mod_row[:, b, 1, :], first_half[:, 1, :])
                ve.tensor_scalar(mod_row[:, b, 2, :], second_half[:, 0, :], 1.0, None, ALU.add)
                for i, (k, src) in enumerate(((0, first_half[:, 0, :]), (3, second_half[:, 1, :]))):
                    n = 4 * (2 * b + i)
                    wait(dve, modrow_step, n)
                    ve.tensor_scalar(gate_sign[:, :], src, 0.0, 2.0, ALU.is_ge, ALU.mult).then_inc(modrow_step, 1)
                    wait(dve, modrow_step, n + 1)
                    ve.scalar_tensor_tensor(gate_abs[:, :], gate_sign[:, :], -1.0, src, ALU.add, ALU.mult)\
                        .then_inc(modrow_step, 1)
                    wait(dve, modrow_step, n + 2)
                    ve.tensor_scalar(gate_size[:, :], gate_abs[:, :], GATE_MIN, None, ALU.max)\
                        .then_inc(modrow_step, 1)
                    wait(dve, modrow_step, n + 3)
                    ve.scalar_tensor_tensor(mod_row[:, b, k, :], gate_sign[:, :], -1.0, gate_size[:, :],
                                            ALU.add, ALU.mult).then_inc(modrow_step, 1)
            dve.wait_ge(modrow_step, 8 * B)
            dve.wait_ge(zero_rows, 1)
            dve.wait_ge(d_small, 16 * N_SMALL)
            ve.tensor_copy(bqk_t[32:33, :], bqk_raw[32:33, :])
            for row in (0, 32):
                for b in range(B):
                    last = TT(bo_g[row:row + 1, b, :], bo_raw[row:row + 1, :], mod_row[row:row + 1, b, 0, :], ALU.mult)
            last.then_inc(small_step, 1)
            dve.wait_ge(small_step, 1)
            ve.tensor_copy(bo_t[32:33, :, :], bo_g[32:33, :, :])
            ve.tensor_copy(b2_hi[0:2 * NE, :], b2_raw[:, :])
            ve.tensor_copy(route_hi[:, :, :], route_raw[:, :, :]).then_inc(small_step, 1)
            dve.wait_ge(small_step, 2)
            ve.tensor_copy(bqk_r[0:1, :], bqk_raw[0:1, :])
            TT(bqk_r[32:33, :], bqk_raw[32:33, :], bqk_t[32:33, :].bitcast(F32), ALU.subtract)
            ve.tensor_copy(bo_r[0:1, :, :], bo_g[0:1, :, :])
            TT(bo_r[32:33, :, :], bo_g[32:33, :, :], bo_t[32:33, :, :].bitcast(F32), ALU.subtract)
            TT(b2_lo[0:2 * NE, :], b2_raw[:, :], b2_hi[0:2 * NE, :].bitcast(F32), ALU.subtract)
            TT(route_lo[:, :, :], route_raw[:, :, :], route_hi[:, :, :].bitcast(F32), ALU.subtract)
            dve.wait_ge(const_ready, 1)
            ve.tensor_copy(sel[:, :, :], sel_f[:, :, :])
            TT(cent_sq[:, :, :], route_raw[:, :, 0:NE], route_raw[:, :, 0:NE], ALU.mult).then_inc(small_ready, 1)

            def split_a(u):
                h = u.h
                wait(dve, a_hf, u.count(1, 1))
                wait(dve, a_v, u.count(1, -1))
                ve.tensor_copy(tr_hi[:, h, :, :], tr_f[:, h, :, :]).then_inc(a_hi, 1)

            def feature_map(u, t):
                h = u.h
                wait(dve, a_exp, u.count(2, t + 1))
                if t == 0:
                    wait(dve, a_kv, u.count(1, -1))
                    wait(dve, a_kst, u.count(2, -1))
                ve.scalar_tensor_tensor(q_sb[:, u.tile(t), :], bank[2 + t][:, 0:E], 1.0, e_sb[:, t, 0:E],
                                        ALU.add, ALU.max)
                ve.scalar_tensor_tensor(k_sb[:, h, t, :], bank[2 + t][:, E:2 * E], 1.0, e_sb[:, t, E:2 * E],
                                        ALU.add, ALU.max).then_inc(a_fm, 1)

            def add_kv(u):
                b = u.batch()
                wait(dve, a_kv, u.count(1, 1))
                wait(dve, a_acc, u.count(1, 0))
                acc = kv_acc[:, b, :, :].rearrange("p c n -> p (c n)")
                TT(acc, acc, bank[6 + u.h][:, 0:E], ALU.add).then_inc(a_acc, 1)

            def step_a(u):
                if u.plus(1):
                    split_a(u.plus(1))
                if u.plus(2):
                    stats_a(u.plus(2))
                feature_map(u, 0)
                feature_map(u, 1)
                if u.plus(-1):
                    add_kv(u.plus(-1))

            dve.wait_ge(acc_zero, 1)
            split_a(u0)
            pipeline(ve, step_a)
            add_kv(Unit(NU // 2 - 1, 1, NU, UPB))

            dve.wait_ge(cent_done, 1)
            ve.tensor_scalar(cent_n2[:, :], bank[6][:, 0:NE], NORM_EPS2, None, ALU.max).then_inc(cent_n2_ready, 1)

            dve.wait_ge(f_ksum, 1)
            for b in range(B):
                ve.tensor_copy(ksum_row[:, b, :], bank[7][:, b * E:(b + 1) * E]).then_inc(f_ksrow, 1)
            dve.wait_ge(f_ksrow, B)
            dve.wait_ge(a_acc, NU)
            for b in range(B):
                if b:
                    dve.wait_ge(f_kvm, b)
                for c in range(NC):
                    last = ve.scalar_tensor_tensor(kv_b[:, c, :], ksum_row[:, b, c * P:(c + 1) * P],
                                                   bv_sb[:, c:c + 1], kv_acc[:, b, c, :], ALU.mult, ALU.add)
                last.then_inc(f_step, 1)
                dve.wait_ge(f_step, 3 * b + 1)
                for c in range(NC):
                    last = TT(kv_m[:, b, c, :], kv_b[:, c, :], head_mask[:, :], ALU.mult)
                last.then_inc(f_kvm, 1)
                dve.wait_ge(f_m, b + 1)
                for c in range(NC):
                    last = TT(m_f[:, b, c, :], bank[4 + b][:, c * E:(c + 1) * E], mod_row[:, b, 0, :], ALU.mult)
                last.then_inc(f_step, 1)
                dve.wait_ge(f_step, 3 * b + 2)
                ve.tensor_copy(m_hi[:, b, :, :], m_f[:, b, :, :]).then_inc(f_step, 1)
                dve.wait_ge(f_step, 3 * b + 3)
                TT(m_lo[:, b, :, :], m_f[:, b, :, :], m_hi[:, b, :, :].bitcast(F32), ALU.subtract)\
                    .then_inc(f_ready, 1)

            def denominators(u):
                h = u.h
                wait(dve, o_prod, u.count(1, 1))
                wait(dve, o_qz, u.count(1, -1))
                ve.tensor_reduce(den[:, h, :, :].rearrange("p t h -> p (t h)"),
                                 prod[:, h, :, :].rearrange("p t (h d) -> p (t h) d", d=D),
                                 axis=AXX, op=ALU.add).then_inc(o_den, 1)
                wait(dve, o_den, u.count(2, 1))
                ve.tensor_scalar(den_e[:, h, :, :], den[:, h, :, :], DEN_EPS, None, ALU.add).then_inc(o_den, 1)
                wait(dve, o_den, u.count(2, 2))
                ve.reciprocal(z[:, h, :, :], den_e[:, h, :, :]).then_inc(o_z, 1)

            def lo_o(u):
                h = u.h
                wait(dve, o_hi, u.count(1, 1))
                TT(tr_lo[:, h, :, :].rearrange("p c n -> p (c n)"), bank[h][:, :],
                   tr_hi[:, h, :, :].rearrange("p c n -> p (c n)").bitcast(F32), ALU.subtract).then_inc(o_lo, 1)

            def add_attention(u):
                wait(dve, o_y, u.count(1, 1))
                xt = x_sb[:, bass.ds(u.tile(0), 2), :]
                TT(xt, xt, bank[2 + u.h][:, :].rearrange("p (t e) -> p t e", t=2), ALU.add).then_inc(o_x1, 1)

            def step_o(u):
                if u.plus(2):
                    denominators(u.plus(2))
                lo_o(u)
                if u.plus(-1):
                    add_attention(u.plus(-1))

            denominators(u0)
            denominators(u0.plus(1))
            pipeline(ve, step_o)
            add_attention(Unit(NU // 2 - 1, 1, NU, UPB))

            dve.wait_ge(d_w1, 32)
            for c in range(NC):
                ve.tensor_copy(w1_hi[:, c, :, :], w1_raw[:, c, :, :]).then_inc(w1_step, 1)
            for c in range(NC):
                dve.wait_ge(w1_step, c + 1)
                last = TT(w1_lo[:, c, :, :], w1_raw[:, c, :, :], w1_hi[:, c, :, :].bitcast(F32), ALU.subtract)
            last.then_inc(w1_ready, 1)
            dve.wait_ge(d_w2, 16)
            ve.tensor_copy(w2_hi[:, :, :], w2_raw[:, :, :]).then_inc(w2_step, 1)
            dve.wait_ge(w2_step, 1)
            TT(w2_lo[:, :, :], w2_raw[:, :, :], w2_hi[:, :, :].bitcast(F32), ALU.subtract).then_inc(w2_ready, 1)

            def stats_e(u):
                def x_ready():
                    wait(dve, o_x1, u.count(1, 1))
                stats_of(u, x_ready, e_st, e_stats, e_rstd)

            def modulate_e(u):
                h, b = u.h, u.batch()
                wait(dve, e_rstd, u.count(1, 1))
                wait(dve, e_tp, u.count(1, -1))
                wait(dve, e_sq, u.count(2, -2))
                for t in range(2):
                    ve.scalar_tensor_tensor(xc[:, t, :], x_sb[:, u.tile(t), :], mv[:, h, t, 0:1],
                                            mod_row[:, b, 2, :], ALU.subtract, ALU.mult).then_inc(e_xc, 1)
                for t in range(2):
                    wait(dve, e_xc, u.count(2, t + 1))
                    last = ve.scalar_tensor_tensor(nat[:, h, t, :], xc[:, t, :], rstd[:, h, t:t + 1],
                                                   mod_row[:, b, 1, :], ALU.mult, ALU.add)
                last.then_inc(e_h, 1)

            def clip_norm(u):
                wait(dve, e_sq, u.count(2, 2))
                wait(dve, e_rn, u.count(1, -1))
                ve.tensor_scalar(h_n2c[:, u.h, :], h_n2[:, u.h, :], NORM_EPS2, None, ALU.max).then_inc(e_n2, 1)

            def lo_e(u):
                h = u.h
                wait(dve, e_hi, u.count(1, 1))
                TT(tr_lo[:, h, :, :].rearrange("p c n -> p (c n)"), bank[0][:, :],
                   tr_hi[:, h, :, :].rearrange("p c n -> p (c n)").bitcast(F32), ALU.subtract).then_inc(e_lo, 1)

            def gate(u, p):
                s = p % 2
                wait(dve, e_gelu, u.count(NP, p + 1))
                wait(dve, e_gb, u.count(NP, p + 1))
                wait(dve, e_hlo, u.count(NP, p - 1))
                TT(hid_g[:, s, :, :].rearrange("p j n -> p (j n)"), hid[:, s, :, :].rearrange("p j n -> p (j n)"),
                   bank[4 + s][:, :], ALU.mult).then_inc(e_mul, 1)

            G = 8

            def gates_a(u):
                wait(dve, e_lgT, u.count(1, 1))
                wait(dve, e_rn, u.count(1, 1))
                lg = bank[1][:, 0:4 * NE].rearrange("p (t k) -> p t k", t=2)
                TT(cosw[:, :, :], lg[:, :, 0:NE],
                   cent_rn[:, :].rearrange("p (o e) -> p o e", o=1).to_broadcast([P, 2, NE]), ALU.mult)\
                    .then_inc(e_gstep, 1)
                wait(dve, e_gstep, u.count(G, 1))
                for t in range(2):
                    last = ve.scalar_tensor_tensor(logit[:, t, :], cosw[:, t, :], h_rn[:, u.h, t:t + 1],
                                                   lg[:, t, NE:2 * NE], ALU.mult, ALU.add)
                last.then_inc(e_gstep, 1)
                wait_alone(dve, met_v, e_gstep, u.count(G, 2))
                for t in range(2):
                    last = ve.max(top[:, t, :], logit[:, t, :])
                last.then_inc(e_gstep, 1)
                wait(dve, e_gstep, u.count(G, 3))
                TT(shifted[:, :, :], logit[:, :, :], top[:, :, 0:1].to_broadcast([P, 2, NE]), ALU.subtract)\
                    .then_inc(e_shift, 1)
                TT(chosen[:, :, :], logit[:, :, :], top[:, :, 1:2].to_broadcast([P, 2, NE]), ALU.is_ge)\
                    .then_inc(e_gstep, 1)

            def gates_b(u):
                wait(dve, e_gstep, u.count(G, 4))
                wait(dve, e_gexp, u.count(1, 1))
                TT(g_sel[:, :, :], g_exp[:, :, :], chosen[:, :, :], ALU.mult).then_inc(e_gstep, 1)
                wait(dve, e_gstep, u.count(G, 5))
                ve.tensor_reduce(g_sum[:, :], g_sel[:, :, :], axis=AXX, op=ALU.add).then_inc(e_gstep, 1)
                wait(dve, e_gstep, u.count(G, 6))
                ve.reciprocal(g_rec[:, :], g_sum[:, :]).then_inc(e_gstep, 1)
                wait(dve, e_gstep, u.count(G, 7))
                TT(g_f[:, :, :], g_sel[:, :, :],
                   g_rec[:, :].rearrange("p (t o) -> p t o", o=1).to_broadcast([P, 2, NE]), ALU.mult)\
                    .then_inc(e_gstep, 1)
                wait(dve, e_gstep, u.count(G, 8))
                ve.tensor_copy(g_hir[:, :, :], g_f[:, :, :]).then_inc(e_gfs, 1)
                wait(dve, e_gfs, u.count(1, 1))
                wait(dve, e_gTp, u.count(1, 0))
                ve.tensor_copy(g_hilo[:, :, 0:NE], g_hir[:, :, :].bitcast(F32))
                TT(g_hilo[:, :, NE:2 * NE], g_f[:, :, :], g_hir[:, :, :].bitcast(F32), ALU.subtract)\
                    .then_inc(e_gnat, 1)

            def keep_gates(u):
                wait(dve, e_gTp, u.count(1, 1))
                wait(dve, e_gb, u.count(NP, -NP))
                ve.tensor_copy(gT[0:2 * NE, u.h, :], bank[1][0:2 * NE, 0:2 * P]).then_inc(e_gT, 1)

            def scale_experts(u):
                b = u.batch()
                wait(dve, e_f2, u.count(NP, NP))
                wait(dve, e_y, u.count(1, 0))
                for t in range(2):
                    last = TT(y_g[:, t, :], bank[6 + t][:, 0:E], mod_row[:, b, 3, :], ALU.mult)
                last.then_inc(e_yg, 1)

            def step_e(u):
                n = u.plus(1)
                keep_gates(u)
                gate(u, 0)
                if n:
                    modulate_e(n)
                if u.plus(-1):
                    scale_experts(u.plus(-1))
                gate(u, 1)
                if n:
                    clip_norm(n)
                    lo_e(n)
                gate(u, 2)
                if u.plus(2):
                    stats_e(u.plus(2))
                if n:
                    gates_a(n)
                gate(u, 3)
                if n:
                    gates_b(n)

            dve.wait_ge(cent_ready, 1)
            stats_e(u0)
            modulate_e(u0)
            clip_norm(u0)
            lo_e(u0)
            stats_e(u0.plus(1))
            gates_a(u0)
            gates_b(u0)
            pipeline(ve, step_e)
            scale_experts(Unit(NU // 2 - 1, 1, NU, UPB))


def kernel(**inputs):
    import numpy as np
    import concourse.bacc as bacc
    from concourse.bass_utils import run_bass_kernel_spmd

    a = {k.replace("L0_", ""): np.asarray(v) for k, v in inputs.items()}
    B, S, E = a["attn_x"].shape
    given = {
        "x": a["attn_x"].reshape(B * S, E),
        "wqkvT": np.concatenate([a["attn_Wq"].T, a["attn_Wk"].T, a["attn_Wv"].T], axis=1),
        "bqk": np.concatenate([a["attn_bq"], a["attn_bk"]]).reshape(1, 2 * E),
        "bvT": a["attn_bv"].reshape(2, E // 2).T,
        "woT": a["attn_Wo"].T,
        "bo": a["attn_bo"].reshape(1, E),
        "w1": a["ffn_w1"],
        "b1T": a["ffn_b1"].T,
        "w2": a["ffn_w2"],
        "b2": a["ffn_b2"],
        "routeT": np.concatenate([a["ffn_centroids"].T, a["ffn_w_route"].T], axis=1),
        "cT": a["c"].T,
        "wmod": a["wmod"],
    }
    nc = bacc.Bacc("TRN2", target_bir_lowering=False, num_devices=1)
    arrays, args = {}, []
    for name, value in given.items():
        value = np.ascontiguousarray(value)
        arrays[f"in_{name}"] = value
        args.append(nc.dram_tensor(f"in_{name}", value.shape, mybir.dt.from_np(value.dtype), kind="ExternalInput").ap())
    out = nc.dram_tensor("out_0", (B * S, E), F32, kind="ExternalOutput").ap()
    adaln_block(nc, *args, out)
    got = run_bass_kernel_spmd(nc, [arrays], core_ids=[0])
    return got.results[0]["out_0"].reshape(B, S, E)
```

```python
import math

import concourse.bass as bass
from concourse import mybir
from contextlib import ExitStack


F32 = mybir.dt.float32
F32R = mybir.dt.float32r
ALU = mybir.AluOpType
ACT = mybir.ActivationFunctionType
AXX = mybir.AxisListType.X

P = 128
LN_EPS = 1e-5
DEN_EPS = 1e-6
NORM_EPS2 = 1e-24
GATE_MIN = 0.25


class Unit:

    def __init__(self, it, h, n_units, per_batch):
        self.it, self.h, self.n_units, self.per_batch = it, h, n_units, per_batch

    def plus(self, d):
        k = self.h + d
        return Unit(self.it + k // 2 if k // 2 else self.it, k % 2, self.n_units, self.per_batch)

    def __bool__(self):
        return not isinstance(self.it, int) or 0 <= 2 * self.it + self.h < self.n_units

    def count(self, n=1, c=0):
        return self.it * (2 * n) + (self.h * n + c)

    def tile(self, t):
        return self.it * 4 + (2 * self.h + t)

    def batch(self):
        return self.it // (self.per_batch // 2)


def wait(eng, sem, value):
    if isinstance(value, int) and value <= 0:
        return
    eng.wait_ge(sem, value)


MODROW_STEPS = 8
N_SMALL = 4


def adaln_block(nc, x, wqkvT, rows, cols, woT, w1, w2, b2, cT, wmod, out):
    S, E = x.shape
    B = cT.shape[1]
    NE, _, HID = w1.shape
    NC = E // P
    NT = S // P
    NU = NT // 2
    UPB = NU // B
    D = 16
    NH = E // D
    assert NC == 2 and HID == P and NE == 8 and B == 2 and UPB % 2 == 0 and NU >= 8
    NP = NE // 2

    ctx = ExitStack()
    with ctx:
        def sb(name, shape, dt=F32):
            return ctx.enter_context(nc.sbuf_tensor(name, shape, dt))

        def sem(name):
            return ctx.enter_context(nc.semaphore(name))

        def unit(u):
            return Unit(u // 2, u % 2, NU, UPB)

        def pipeline(eng, step, start, loop_from, loop_to):
            for u in range(start, loop_from):
                step(unit(u))
            with eng.Fori(loop_from // 2, loop_to // 2) as it:
                for h in range(2):
                    step(Unit(it, h, NU, UPB))
            for u in range(loop_to, NU):
                step(unit(u))

        x_sb = sb("x_sb", [P, NT, E])
        q_sb = sb("q_sb", [P, NT, E])
        ident = sb("ident", [P, P])
        ones_f = sb("ones_f", [P, P])
        ones_r = sb("ones_r", [P, P], F32R)
        head_mask = sb("head_mask", [P, P])
        sel = sb("sel", [P, NE, P], F32R)
        minus_half = sb("minus_half", [P, NE])
        euler = sb("euler", [P, 2 * NE])

        c_sb = sb("c_sb", [P, NC, B])
        c_exp = sb("c_exp", [P, NC, B])
        c_den = sb("c_den", [P, NC, B])
        c_rec = sb("c_rec", [P, NC, B])
        c_silu = sb("c_silu", [P, NC, B])
        c_rep = sb("c_rep", [P, NC, B, P])
        early = sb("early", [P, NC * 6 * E])
        wmod_sb = early[:, :].rearrange("p (c n) -> p c n", c=NC)
        prod = early[:, 0:2 * E].rearrange("p (t e) -> p t e", t=2)
        mod_col = sb("mod_col", [P, 4, B])
        mod_row = sb("mod_row", [P, B, 4, E])

        gate_sign, gate_abs, gate_size = (q_sb[:, 10 + i, :] for i in range(3))

        wm_raw = sb("wm_raw", [P, NC * 3 * E])
        wm_hi = sb("wm_hi", [P, NC * 3 * E], F32R)
        wm_lo = sb("wm_lo", [P, NC * 3 * E], F32R)
        wqkv_raw, wqkv_hi, wqkv_lo = (m[:, :].rearrange("p (c n) -> p c n", c=NC) for m in (wm_raw, wm_hi, wm_lo))
        m_f, m_hi, m_lo = (m[:, 0:B * NC * E].rearrange("p (b c n) -> p b c n", b=B, c=NC)
                           for m in (wm_raw, wm_hi, wm_lo))
        qz_hi, qz_lo = (m[:, B * NC * E:].rearrange("p (c n) -> p c n", c=NC) for m in (wm_hi, wm_lo))
        early_q = q_sb[:, 0:10, :].rearrange("p t e -> p (t e)")
        rows_raw = early_q[0:33, 0:3 * E]
        bqk_raw, bo_raw = rows_raw[:, 0:2 * E], rows_raw[:, 2 * E:3 * E]
        bqk_t = early_q[0:33, 3 * E:5 * E].bitcast(F32R)
        bo_g = early_q[0:33, 5 * E:7 * E].rearrange("p (b e) -> p b e", b=B)
        bo_t = early_q[0:33, 7 * E:9 * E].bitcast(F32R).rearrange("p (b e) -> p b e", b=B)
        b2_raw = early_q[0:2 * NE, 9 * E:10 * E]
        bqk_r = sb("bqk_r", [P, 2 * E], F32R)
        cols_sb = sb("cols_sb", [P, NC * 2 * NE + NC + NE])
        route_raw = cols_sb[:, 0:NC * 2 * NE].rearrange("p (c n) -> p c n", c=NC)
        bv_sb = cols_sb[:, NC * 2 * NE:NC * 2 * NE + NC]
        b1_sb = cols_sb[:, NC * 2 * NE + NC:]
        wo_sb = sb("wo_sb", [P, NC, E])
        bo_r = sb("bo_r", [P, B, E], F32R)
        w_raw = q_sb[:, NT - 2 * NE:NT, :]
        w1_raw = w_raw[:, 0:NE, :].rearrange("p (c g) (k j) -> p c (g k) j", c=NC, k=E // HID)
        w2_raw = w_raw[:, NE:2 * NE, :]
        w_hi = sb("w_hi", [P, 2 * NE, E], F32R)
        w_lo = sb("w_lo", [P, 2 * NE, E], F32R)
        w1_hi, w1_lo = (m[:, 0:NE, :].rearrange("p (c g) (k j) -> p c (g k) j", c=NC, k=E // HID) for m in (w_hi, w_lo))
        w2_hi, w2_lo = (m[:, NE:2 * NE, :] for m in (w_hi, w_lo))
        b2_hi = sb("b2_hi", [P, E], F32R)
        b2_lo = sb("b2_lo", [P, E], F32R)
        route_hi = sb("route_hi", [P, NC, 2 * NE], F32R)
        route_lo = sb("route_lo", [P, NC, 2 * NE], F32R)
        cent_sq = sb("cent_sq", [P, NC, NE])
        cent_n2 = sb("cent_n2", [P, NE])
        cent_rn = sb("cent_rn", [P, NE])

        stats = sb("stats", [P, 2, 2, 6])
        mv = sb("mv", [P, 2, 2, 2])
        var_eps = sb("var_eps", [P, 2, 2])
        neg_mean = sb("neg_mean", [P, 2, 2])
        rstd = sb("rstd", [P, 2, 2])
        neg_mr = sb("neg_mr", [P, 2, 2])
        nat = sb("nat", [P, 2, 2, E])
        tr_f = sb("tr_f", [P, 2, NC, 2 * P])
        tr_hi = sb("tr_hi", [P, 2, NC, 2 * P], F32R)
        tr_lo = sb("tr_lo", [P, 2, NC, 2 * P], F32R)
        e_sb = sb("e_sb", [P, 2, 2 * E])
        sel_f = e_sb[:, :, :].rearrange("p t (e q) -> p (t e) q", q=P)
        qz = e_sb[:, 0, :].rearrange("p (t e) -> p t e", t=2)
        k_sb = sb("k_sb", [P, 2, 2, E])
        xc, y_g = k_sb[:, 0, :, :], k_sb[:, 1, :, :]
        v_sb = sb("v_sb", [P, 2, 2, E])
        sq = v_sb[:, 0, 0, :]
        lg_t = v_sb[0:2 * NE, 1, 0, :]
        k_sum = sb("k_sum", [P, B, E])
        kv_acc = sb("kv_acc", [P, B, NC, P])
        ksum_row = sb("ksum_row", [P, B, E])
        kv_b = tr_f[:, 0, 0, :].rearrange("p (c n) -> p c n", c=NC)
        kv_m = tr_f[:, 1, :, :].rearrange("p b (c n) -> p b c n", c=NC)
        den = sb("den", [P, 2, NH])
        den_e = sb("den_e", [P, 2, NH])
        z = sb("z", [P, 2, NH])
        h_n2 = sb("h_n2", [P, 2, 2])
        h_n2c = sb("h_n2c", [P, 2, 2])
        h_rn = sb("h_rn", [P, 2, 2])
        cosw = sb("cosw", [P, 2, NE])
        logit = sb("logit", [P, 2, NE])
        top = sb("top", [P, 2, 8])
        shifted = sb("shifted", [P, 2, NE])
        chosen = sb("chosen", [P, 2, NE])
        g_exp = sb("g_exp", [P, 2, NE])
        g_sel = sb("g_sel", [P, 2, NE])
        g_sum = sb("g_sum", [P, 2])
        g_rec = sb("g_rec", [P, 2])
        g_f = sb("g_f", [P, 2, NE])
        g_hilo = sb("g_hilo", [P, 2, 2 * NE], F32R)
        gT = sb("gT", [P, 2, 2 * P], F32R)
        hid = sb("hid", [P, 2, 2, 2 * P])
        hid_g = sb("hid_g", [P, 2, 2, 2 * P])
        hid_hi = sb("hid_hi", [P, 2, 2, 2 * P], F32R)
        hid_lo = sb("hid_lo", [P, 2, 2, 2 * P], F32R)

        bank = [ctx.enter_context(nc.psum_tensor(f"bank{i}", [P, 512], F32)) for i in range(8)]
        chunks = "p (c n) -> p c n"

        d_c = sem("d_c"); d_wmod = [sem(f"d_wmod{k}") for k in range(3)]; d_qkv = sem("d_qkv"); d_wo = sem("d_wo")
        d_w = sem("d_w"); d_small = sem("d_small")
        x_in = [sem(f"x_in{h}") for h in range(2)]
        y_out = [sem(f"y_out{h}") for h in range(2)]
        const_step = sem("const_step"); const_ready = sem("const_ready")
        c_exp_ready = sem("c_exp_ready"); silu_step = sem("silu_step"); c_rep_ready = sem("c_rep_ready")
        modcol_done = sem("modcol_done"); modcol_ready = sem("modcol_ready")
        modrow_done = sem("modrow_done"); modrow_step = sem("modrow_step")
        qkv_step = sem("qkv_step"); qkv_ready = sem("qkv_ready")
        zero_rows = sem("zero_rows"); sel_ready = sem("sel_ready"); cent_done = sem("cent_done"); cent_n2_ready = sem("cent_n2_ready")
        cent_ready = sem("cent_ready")
        w_hi_done = sem("w_hi_done"); w_ready = sem("w_ready")
        small_step = sem("small_step")
        small_ready = sem("small_ready"); bqk_step = sem("bqk_step"); bqk_ready = sem("bqk_ready")

        a_st = sem("a_st"); a_stats = sem("a_stats"); a_pow = sem("a_pow"); a_rstd = sem("a_rstd")
        a_xn = sem("a_xn"); a_tp = sem("a_tp"); a_hf = sem("a_hf"); a_hi = sem("a_hi"); a_lo = sem("a_lo")
        a_qk = sem("a_qk"); a_v = sem("a_v"); a_exp = sem("a_exp"); a_vs = sem("a_vs"); a_neg = sem("a_neg")
        a_fm = sem("a_fm"); a_ks = sem("a_ks"); a_kst = sem("a_kst"); a_kv = sem("a_kv"); a_acc = sem("a_acc")
        acc_zero = sem("acc_zero")

        f_ksum = sem("f_ksum"); f_ksrow = sem("f_ksrow"); f_step = sem("f_step"); f_kvm = sem("f_kvm")
        f_m = sem("f_m"); f_ready = sem("f_ready")

        o_prod = sem("o_prod"); o_den = sem("o_den"); o_z = sem("o_z"); o_qz = sem("o_qz"); o_tp = sem("o_tp")
        o_hi = sem("o_hi"); o_lo = sem("o_lo"); o_y = sem("o_y"); o_x1 = sem("o_x1")

        e_st = sem("e_st"); e_stats = sem("e_stats"); e_rstd = sem("e_rstd"); e_xc = sem("e_xc")
        e_h = sem("e_h"); e_sq = sem("e_sq"); e_n2 = sem("e_n2"); e_rn = sem("e_rn")
        e_tp = sem("e_tp"); e_hi = sem("e_hi"); e_lo = sem("e_lo")
        e_route = sem("e_route"); e_lgs = sem("e_lgs"); e_lgT = sem("e_lgT"); e_gstep = sem("e_gstep")
        e_shift = sem("e_shift"); e_gexp = sem("e_gexp"); e_gnat = sem("e_gnat"); e_gTp = sem("e_gTp")
        e_gT = sem("e_gT")
        e_f1 = sem("e_f1"); e_gb = sem("e_gb"); e_gelu = sem("e_gelu"); e_mul = sem("e_mul")
        e_hhi = sem("e_hhi"); e_hlo = sem("e_hlo"); e_f2 = sem("e_f2"); e_yg = sem("e_yg"); e_y = sem("e_y")

        met_v = sem("met_v"); met_g = sem("met_g"); met_t = sem("met_t")

        def wait_alone(eng, met, on, value):
            wait(eng, on, value)
            if not isinstance(value, int):
                eng.sem_inc(met, 1)

        block = ctx.enter_context(nc.Block())

        @block.sync
        def _(sp):
            def load_x(it, h):
                t = it * 4 + 2 * h
                wait(sp, x_in[h], it * 16)
                sp.dma_start(x_sb[:, bass.ds(t, 2), :], x_tiles[:, bass.ds(t, 2), :]).then_inc(x_in[h], 16)

            x_tiles = x.rearrange("(t p) e -> p t e", p=P)
            out_tiles = out.rearrange("(t p) e -> p t e", p=P)
            small = [(rows_raw[0:1, :], rows), (rows_raw[32:33, :], rows), (cols_sb[:, :], cols),
                     (b2_raw[:, :], b2)]
            assert len(small) == N_SMALL
            load_x(0, 0)
            sp.dma_start(wqkv_raw[:, :, :], wqkvT.rearrange("(c p) n -> p c n", p=P)).then_inc(d_qkv, 16)
            for to, of in small:
                sp.dma_start(to, of).then_inc(d_small, 16)
            load_x(0, 1)
            load_x(1, 0)
            load_x(1, 1)
            sp.dma_start(w1_raw[:, 0, :, :], w1[:, 0:P, :].rearrange("e p j -> p e j")).then_inc(d_w, 16)
            sp.dma_start(w1_raw[:, 1, :, :], w1[:, P:2 * P, :].rearrange("e p j -> p e j")).then_inc(d_w, 16)
            sp.dma_start(w2_raw, w2.rearrange("e p d -> p e d")).then_inc(d_w, 16)
            sp.dma_start(wo_sb[:, :, :], woT.rearrange("(c p) n -> p c n", p=P)).then_inc(d_wo, 16)
            with sp.Fori(2, NU // 2) as it:
                for h in range(2):
                    load_x(it, h)

            def store(u):
                wait(sp, e_y, u.count(1, 1))
                sp.dma_start(out_tiles[:, bass.ds(u.tile(0), 2), :],
                             x_sb[:, bass.ds(u.tile(0), 2), :]).then_inc(y_out[u.h], 16)

            pipeline(sp, store, 0, 2, NU - 2)
            for h in range(2):
                sp.wait_ge(y_out[h], 16 * (NU // 2))

        @block.gpsimd
        def _(pool):
            gp = nc.gpsimd
            gp.memset(ident[:, :], 0.0).then_inc(const_step, 1)
            gp.memset(sel_f[:, :, :], 0.0).then_inc(const_step, 1)
            gp.memset(head_mask[:, :], 1.0).then_inc(const_step, 1)
            gp.memset(minus_half[:, :], -0.5)
            gp.memset(euler[:, :], math.e)
            gp.memset(ones_f[:, :], 1.0)
            pool.wait_ge(const_step, 3)
            gp.affine_select(out=ident[:, :], in_=ident[:, :], compare_op=ALU.not_equal, fill=1.0,
                             base=0, pattern=[[-1, P]], channel_multiplier=1)
            gp.affine_select(out=sel_f[:, :, :], in_=sel_f[:, :, :], compare_op=ALU.not_equal, fill=1.0,
                             base=0, pattern=[[-1, NE], [0, P]], channel_multiplier=1).then_inc(const_step, 1)
            heads = head_mask[:, :].rearrange("p (h d) -> p h d", d=D)
            gp.affine_select(out=heads, in_=heads, compare_op=ALU.is_ge, fill=0.0,
                             base=0, pattern=[[-D, P // D], [0, D]], channel_multiplier=1).then_inc(const_step, 1)
            pool.wait_ge(const_step, 5)
            gp.affine_select(out=sel_f[:, :, :], in_=sel_f[:, :, :], compare_op=ALU.not_equal, fill=1.0,
                             base=-NE, pattern=[[-1, NE], [0, P]], channel_multiplier=1)
            gp.affine_select(out=heads, in_=heads, compare_op=ALU.is_ge, fill=0.0,
                             base=D - 1, pattern=[[D, P // D], [0, D]], channel_multiplier=-1)\
              .then_inc(const_ready, 1)
            gp.memset(k_sum[:, :, :], 0.0).then_inc(a_kst, 1)

            def rstd_a(u):
                h = u.h
                wait(pool, a_stats, u.count(1, 1))
                wait(pool, a_xn, u.count(1, -1))
                gp.tensor_tensor(rstd[:, h, :], var_eps[:, h, :], minus_half[:, 0:2], ALU.pow).then_inc(a_pow, 1)
                wait(pool, a_pow, u.count(1, 1))
                gp.tensor_tensor(neg_mr[:, h, :], neg_mean[:, h, :], rstd[:, h, :], ALU.mult).then_inc(a_rstd, 1)

            def split_lo(u):
                h = u.h
                wait(pool, a_hi, u.count(1, 1))
                wait(pool, a_v, u.count(1, -1))
                gp.tensor_tensor(tr_lo[:, h, :, :], tr_f[:, h, :, :], tr_hi[:, h, :, :].bitcast(F32), ALU.subtract)\
                  .then_inc(a_lo, 1)

            def add_ksum(u):
                b = u.batch()
                for t in range(2):
                    wait(pool, a_fm, u.count(2, t + 1))
                    wait_alone(pool, met_g, a_kst, u.count(2, t + 1))
                    add = gp.tensor_tensor(k_sum[:, b, :], k_sum[:, b, :], k_sb[:, u.h, t, :], ALU.add)
                    add.then_inc(a_kst, 1)

            def step_a(u):
                if u.plus(2):
                    rstd_a(u.plus(2))
                if u.plus(1):
                    split_lo(u.plus(1))
                if u.plus(-1):
                    add_ksum(u.plus(-1))

            u0 = unit(0)
            rstd_a(u0)
            rstd_a(u0.plus(1))
            split_lo(u0)
            pipeline(gp, step_a, 0, 2, NU - 2)
            add_ksum(unit(NU - 1))

            pool.wait_ge(cent_n2_ready, 1)
            gp.tensor_tensor(cent_rn[:, :], cent_n2[:, :], minus_half[:, :], ALU.pow).then_inc(cent_ready, 1)

            def make_prod(u):
                if isinstance(u.it, int):
                    pool.wait_ge(f_ksrow, B)
                wait_alone(pool, met_g, o_z, u.count(1, 0))
                gp.tensor_tensor(prod[:, :, :], q_sb[:, bass.ds(u.tile(0), 2), :],
                                 ksum_row[:, bass.ds(u.batch(), 1), :].to_broadcast([P, 2, E]),
                                 ALU.mult).then_inc(o_prod, 1)

            def make_qz(u):
                wait(pool, o_z, u.count(1, 1))
                wait_alone(pool, met_g, o_tp, u.count(1, 0))
                q4 = q_sb[:, bass.ds(u.tile(0), 2), :].rearrange("p t (h d) -> p (t h) d", d=D)
                n4 = qz[:, :, :].rearrange("p t (h d) -> p (t h) d", d=D)
                z4 = z[:, :, :].rearrange("p t (h o) -> p (t h) o", o=1).to_broadcast([P, 2 * NH, D])
                gp.tensor_tensor(n4, q4, z4, ALU.mult).then_inc(o_qz, 1)

            def rstd_e(u):
                wait(pool, e_stats, u.count(1, 1))
                wait(pool, e_h, u.count(1, -1))
                gp.tensor_tensor(rstd[:, u.h, :], var_eps[:, u.h, :], minus_half[:, 0:2], ALU.pow)\
                  .then_inc(e_rstd, 1)

            def norm_e(u):
                wait(pool, e_n2, u.count(1, 1))
                wait(pool, e_gnat, u.count(1, -1))
                gp.tensor_tensor(h_rn[:, u.h, :], h_n2c[:, u.h, :], minus_half[:, 0:2], ALU.pow)\
                  .then_inc(e_rn, 1)

            def lo_e(u, p):
                s = p % 2
                wait(pool, e_hhi, u.count(NP, p + 1))
                wait(pool, e_f2, u.count(NP, p - 1))
                gp.tensor_tensor(hid_lo[:, s, :, :], hid_g[:, s, :, :], hid_hi[:, s, :, :].bitcast(F32),
                                 ALU.subtract).then_inc(e_hlo, 1)

            def exp_gates(u):
                wait_alone(pool, met_g, e_shift, u.count(1, 1))
                gp.tensor_tensor(g_exp[:, :, :].rearrange("p t e -> p (t e)"), euler[:, :],
                                 shifted[:, :, :].rearrange("p t e -> p (t e)"), ALU.pow).then_inc(e_gexp, 1)

            def add_experts(u):
                wait_alone(pool, met_g, e_yg, u.count(1, 1))
                xt = x_sb[:, bass.ds(u.tile(0), 2), :]
                gp.tensor_tensor(xt, xt, y_g[:, :, :], ALU.add).then_inc(e_y, 1)

            def step_e(u):
                if u.plus(4):
                    make_prod(u.plus(4))
                if u.plus(1):
                    norm_e(u.plus(1))
                if u:
                    lo_e(u, 0)
                if u.plus(-1):
                    add_experts(u.plus(-1))
                if u:
                    lo_e(u, 1)
                if u.plus(1):
                    exp_gates(u.plus(1))
                if u.plus(4):
                    make_qz(u.plus(4))
                if u:
                    lo_e(u, 2)
                if u:
                    lo_e(u, 3)
                if u.plus(3):
                    rstd_e(u.plus(3))

            pipeline(gp, step_e, -4, 2, NU - 4)
            add_experts(unit(NU - 1))

        @block.scalar
        def _(act):
            ac = nc.scalar
            wmod_chunks = wmod.rearrange("(c p) n -> p c n", p=P)
            act.dma_start(c_sb[:, :, :], cT.rearrange("(c p) b -> p c b", p=P)).then_inc(d_c, 16)
            for k in range(3):
                cols_k = slice(k * 2 * E, (k + 1) * 2 * E)
                act.dma_start(wmod_sb[:, :, cols_k], wmod_chunks[:, :, cols_k]).then_inc(d_wmod[k], 16)

            act.wait_ge(d_c, 16)
            ac.activation(c_exp[:, :, :], c_sb[:, :, :], ACT.Exp, scale=-1.0).then_inc(c_exp_ready, 1)

            def normalise(u):
                wait(act, a_rstd, u.count(1, 1))
                wait(act, a_tp, u.count(1, -1))
                for t in range(2):
                    last = ac.activation(nat[:, u.h, t, :], x_sb[:, u.tile(t), :], ACT.Identity,
                                         bias=neg_mr[:, u.h, t:t + 1], scale=rstd[:, u.h, t:t + 1])
                last.then_inc(a_xn, 1)

            def modulate(u, b):
                wait(act, a_tp, u.count(1, 1))
                wait(act, a_lo, u.count(1, -1))
                tp = bank[u.h][:, :].rearrange(chunks, c=NC)
                for c in range(NC):
                    last = ac.activation(tr_f[:, u.h, c, :], tp[:, c, :], ACT.Identity,
                                         bias=mod_col[:, c, b:b + 1] if isinstance(b, int) else mod_col[:, c, bass.ds(b, 1)],
                                         scale=mod_col[:, 2 + c, b:b + 1] if isinstance(b, int) else mod_col[:, 2 + c, bass.ds(b, 1)])
                last.then_inc(a_hf, 1)

            def negative_part(u, t):
                wait(act, a_qk, u.count(2, t + 1))
                if isinstance(u.it, int) and u.it == 0:
                    act.wait_ge(sel_ready, 1)
                ac.activation(e_sb[:, t, :], bank[2 + t][:, :], ACT.Relu, scale=-1.0).then_inc(a_neg, 1)

            def exp_qk(u, t):
                wait(act, a_neg, u.count(2, t + 1))
                ac.activation(e_sb[:, t, :], e_sb[:, t, :], ACT.Exp, scale=-1.0).then_inc(a_exp, 1)

            def keep_v(u):
                wait(act, a_v, u.count(1, 1))
                wait(act, a_kv, u.count(1, -1))
                ac.activation(v_sb[:, u.h, :, :].rearrange("p t e -> p (t e)"), bank[4 + u.h][:, :], ACT.Copy)\
                  .then_inc(a_vs, 1)

            def step_a(u):
                negative_part(u, 0)
                if u.plus(1):
                    modulate(u.plus(1), u.plus(1).batch())
                exp_qk(u, 0)
                negative_part(u, 1)
                exp_qk(u, 1)
                if u.plus(2):
                    normalise(u.plus(2))
                keep_v(u)

            u0 = unit(0)
            normalise(u0)
            act.wait_ge(modcol_ready, 1)
            modulate(u0, 0)
            normalise(u0.plus(1))
            pipeline(ac, step_a, 0, 2, NU - 2)

            def hi_o(u):
                wait(act, o_tp, u.count(1, 1))
                wait(act, o_y, u.count(2, 0))
                ac.activation(qz_hi.rearrange("p c n -> p (c n)"), bank[0][:, :], ACT.Copy).then_inc(o_hi, 1)

            def square(u):
                wait(act, e_h, u.count(1, 1))
                wait(act, e_n2, u.count(1, -1))
                for t in range(2):
                    wait(act, e_sq, u.count(2, t))
                    ac.activation(sq[:, :], nat[:, u.h, t, :], ACT.Square,
                                  accum_out=h_n2[:, u.h, t:t + 1]).then_inc(e_sq, 1)

            def hi_e(u):
                wait(act, e_tp, u.count(1, 1))
                wait(act, e_f1, u.count(NP, -NP))
                ac.activation(tr_hi[:, u.h, :, :].rearrange("p c n -> p (c n)"), bank[0][:, :], ACT.Copy)\
                  .then_inc(e_hi, 1)

            def keep_logits(u):
                wait(act, e_route, u.count(1, 1))
                ac.activation(lg_t[:, :], bank[1][0:2 * NE, 0:2 * P], ACT.Copy).then_inc(e_lgs, 1)

            def keep_gates(u):
                wait(act, e_gTp, u.count(1, 1))
                wait(act, e_gb, u.count(NP, -NP))
                ac.activation(gT[0:2 * NE, u.h, :], bank[1][0:2 * NE, 0:2 * P], ACT.Copy).then_inc(e_gT, 1)

            def gelu(u, p):
                s = p % 2
                wait(act, e_f1, u.count(NP, p + 1))
                wait(act, e_mul, u.count(NP, p - 1))
                for j in range(2):
                    e = 2 * p + j
                    last = ac.activation(hid[:, s, j, :], bank[2 + s][:, 2 * P * j:2 * P * (j + 1)], ACT.Gelu,
                                         bias=b1_sb[:, e:e + 1])
                last.then_inc(e_gelu, 1)

            def hi_hid(u, p):
                s = p % 2
                wait(act, e_mul, u.count(NP, p + 1))
                wait(act, e_f2, u.count(NP, p - 1))
                ac.activation(hid_hi[:, s, :, :].rearrange("p j n -> p (j n)"),
                              hid_g[:, s, :, :].rearrange("p j n -> p (j n)"), ACT.Copy).then_inc(e_hhi, 1)

            def step_e(u):
                n = u.plus(1)
                if u:
                    gelu(u, 0)
                if u.plus(3):
                    hi_o(u.plus(3))
                if u:
                    hi_hid(u, 0)
                if n:
                    keep_logits(n)
                if u:
                    gelu(u, 1)
                    hi_hid(u, 1)
                    gelu(u, 2)
                    hi_hid(u, 2)
                if u.plus(2):
                    square(u.plus(2))
                if u:
                    gelu(u, 3)
                if u.plus(2):
                    hi_e(u.plus(2))
                if u:
                    hi_hid(u, 3)
                if n:
                    keep_gates(n)

            pipeline(ac, step_e, -3, 2, NU - 4)

        @block.tensor
        def _(pe):
            te = nc.tensor

            def mm3(out_ap, l_hi, l_lo, r_hi, r_lo, start, stop):
                te.matmul(out_ap, l_hi, r_hi, start=start, stop=False)
                te.matmul(out_ap, l_hi, r_lo, start=False, stop=False)
                return te.matmul(out_ap, l_lo, r_hi, start=False, stop=stop)

            def transposes(of, to):
                dst = to[:, :].rearrange(chunks, c=NC)
                for c in range(NC):
                    for t in range(2):
                        last = te.transpose(dst[:, c, t * P:(t + 1) * P], of[:, t, c * P:(c + 1) * P],
                                            ident[:, :])
                return last

            def tp_a(u):
                wait(pe, a_xn, u.count(1, 1))
                wait(pe, a_hf, u.count(1, -1))
                transposes(nat[:, u.h, :, :], bank[u.h]).then_inc(a_tp, 1)

            def qk(u, t):
                h = u.h
                if t == 0:
                    wait(pe, a_lo, u.count(1, 1))
                tok = slice(t * P, (t + 1) * P)
                wait(pe, a_fm, u.count(2, t - 1))
                te.matmul(bank[2 + t][:, :], ones_r[:, :], bqk_r[:, :], start=True, stop=False)
                for c in range(NC):
                    last = mm3(bank[2 + t][:, :], tr_hi[:, h, c, tok], tr_lo[:, h, c, tok],
                               wqkv_hi[:, c, 0:2 * E], wqkv_lo[:, c, 0:2 * E], False, c == NC - 1)
                last.then_inc(a_qk, 1)

            def v(u):
                h = u.h
                wait(pe, a_vs, u.count(1, -1))
                for t in range(2):
                    tok = slice(t * P, (t + 1) * P)
                    for c in range(NC):
                        last = mm3(bank[4 + h][:, t * E:(t + 1) * E], tr_hi[:, h, c, tok], tr_lo[:, h, c, tok],
                                   wqkv_hi[:, c, 2 * E:3 * E], wqkv_lo[:, c, 2 * E:3 * E], c == 0, c == NC - 1)
                last.then_inc(a_v, 1)

            def kv(u):
                h = u.h
                wait(pe, a_fm, u.count(2, 2))
                wait(pe, a_vs, u.count(1, 1))
                wait(pe, a_acc, u.count(1, -1))
                if isinstance(u.it, int) and u.it == 0:
                    pe.wait_ge(modrow_step, MODROW_STEPS * B)
                for c in range(NC):
                    f = slice(c * P, (c + 1) * P)
                    for t in range(2):
                        last = te.matmul(bank[6 + h][:, f], v_sb[:, h, t, f], k_sb[:, h, t, f],
                                         start=(t == 0), stop=(t == 1))
                last.then_inc(a_kv, 1)

            def step_a(u):
                qk(u, 0)
                if u.plus(1):
                    tp_a(u.plus(1))
                qk(u, 1)
                v(u)
                if u.plus(-1):
                    kv(u.plus(-1))

            u0 = unit(0)
            pe.wait_ge(const_ready, 1)
            tp_a(u0)
            pe.wait_ge(d_wmod[0], 16)
            pe.wait_ge(c_rep_ready, 1)
            for k in range(4):
                for c in range(NC):
                    last = te.matmul(bank[5][:, k * B:(k + 1) * B], wmod_sb[:, c, k * P:(k + 1) * P],
                                     c_silu[:, c, :], start=(c == 0), stop=(c == NC - 1))
            last.then_inc(modcol_done, 1)

            def mod_rows(b):
                wait(pe, modrow_step, MODROW_STEPS * b)
                for k in range(2):
                    pe.wait_ge(d_wmod[1 + k], 16)
                    for c in range(NC):
                        last = te.matmul(bank[6 + k][:, :], c_rep[:, c, b, :],
                                         wmod_sb[:, c, 2 * E * (k + 1):2 * E * (k + 2)],
                                         start=(c == 0), stop=(c == NC - 1))
                last.then_inc(modrow_done, 1)

            mod_rows(0)
            pe.wait_ge(qkv_ready, 1)
            pe.wait_ge(bqk_ready, 1)
            step_a(u0)
            mod_rows(1)
            pipeline(te, step_a, 1, 2, NU - 2)
            kv(unit(NU - 1))

            pe.wait_ge(a_acc, NU)
            pe.wait_ge(small_ready, 1)
            for c in range(NC):
                last = te.matmul(bank[6][:, 0:NE], ones_f[:, :], cent_sq[:, c, :], start=(c == 0), stop=(c == NC - 1))
            last.then_inc(cent_done, 1)
            pe.wait_ge(a_kst, 2 * NU + 1)
            for b in range(B):
                last = te.matmul(bank[7][:, b * E:(b + 1) * E], ones_f[:, :], k_sum[:, b, :], start=True, stop=True)
            last.then_inc(f_ksum, 1)
            pe.wait_ge(d_wo, 16)
            for b in range(B):
                pe.wait_ge(f_kvm, b + 1)
                for c in range(NC):
                    last = te.matmul(bank[4 + b][:, c * E:(c + 1) * E], kv_m[:, b, c, :], wo_sb[:, c, :],
                                     start=True, stop=True)
                last.then_inc(f_m, 1)

            def tp_o(u):
                wait(pe, o_qz, u.count(1, 1))
                wait(pe, o_x1, u.count(1, 0))
                wait(pe, e_lo, u.count(1, -1))
                transposes(qz[:, :, :], bank[0]).then_inc(o_tp, 1)

            def attend(u, t):
                b = u.batch()
                wait(pe, o_lo, u.count(1, 1))
                tok = slice(t * P, (t + 1) * P)
                to = bank[0][:, t * E:(t + 1) * E]
                te.matmul(to, ones_r[:, :], bo_r[:, b, :], start=True, stop=False)
                for c in range(NC):
                    last = mm3(to, qz_hi[:, c, tok], qz_lo[:, c, tok], m_hi[:, b, c, :], m_lo[:, b, c, :],
                               False, c == NC - 1)
                last.then_inc(o_y, 1)

            pe.wait_ge(f_ready, B)

            def tp_e(u):
                wait(pe, e_h, u.count(1, 1))
                if u.plus(1):
                    wait(pe, o_x1, u.count(1, 2))
                transposes(nat[:, u.h, :, :], bank[0]).then_inc(e_tp, 1)

            def route(u):
                h = u.h
                wait(pe, e_lo, u.count(1, 1))
                wait(pe, e_gT, u.count(1, 0))
                for c in range(NC):
                    last = mm3(bank[1][0:2 * NE, 0:2 * P], route_hi[:, c, :], route_lo[:, c, :],
                               tr_hi[:, h, c, :], tr_lo[:, h, c, :], c == 0, c == NC - 1)
                last.then_inc(e_route, 1)

            def tp_logits(u):
                wait_alone(pe, met_t, e_lgs, u.count(1, 1))
                for t in range(2):
                    last = te.transpose(bank[1][:, t * 2 * NE:(t + 1) * 2 * NE], lg_t[:, t * P:(t + 1) * P],
                                        ident[0:2 * NE, 0:2 * NE])
                last.then_inc(e_lgT, 1)

            def tp_gates(u):
                wait(pe, e_gnat, u.count(1, 1))
                for t in range(2):
                    last = te.transpose(bank[1][0:2 * NE, t * P:(t + 1) * P], g_hilo[:, t, :].bitcast(F32), ident[:, :])
                last.then_inc(e_gTp, 1)

            def first(u, p):
                h, s = u.h, p % 2
                wait(pe, e_gelu, u.count(NP, p - 1))
                for j in range(2):
                    e = 2 * p + j
                    to = bank[2 + s][:, 2 * P * j:2 * P * (j + 1)]
                    for c in range(NC):
                        last = mm3(to, w1_hi[:, c, e, :], w1_lo[:, c, e, :], tr_hi[:, h, c, :], tr_lo[:, h, c, :],
                                   c == 0, c == NC - 1)
                last.then_inc(e_f1, 1)

            def spread_gates(u, p):
                s = p % 2
                if p == 0:
                    wait(pe, e_gT, u.count(1, 1))
                wait(pe, e_mul, u.count(NP, p - 1))
                for j in range(2):
                    last = te.matmul(bank[4 + s][:, 2 * P * j:2 * P * (j + 1)], sel[:, 2 * p + j, :], gT[:, u.h, :],
                                     start=True, stop=True)
                last.then_inc(e_gb, 1)

            def second(u, p):
                s = p % 2
                wait(pe, e_hlo, u.count(NP, p + 1))
                if p == 0:
                    wait(pe, e_yg, u.count(1, 0))
                for t in range(2):
                    tok = slice(t * P, (t + 1) * P)
                    to = bank[6 + t][:, 0:E]
                    if p == 0:
                        te.matmul(to, gT[:, u.h, tok], b2_hi[:, :], start=True, stop=False)
                        te.matmul(to, gT[:, u.h, tok], b2_lo[:, :], start=False, stop=False)
                    for j in range(2):
                        e = 2 * p + j
                        last = mm3(to, hid_hi[:, s, j, tok], hid_lo[:, s, j, tok], w2_hi[:, e, :],
                                   w2_lo[:, e, :], False, p == NP - 1 and j == 1)
                last.then_inc(e_f2, 1)

            def step_e(u):
                n = u.plus(1)
                if u:
                    first(u, 0)
                    spread_gates(u, 0)
                if u.plus(3):
                    tp_o(u.plus(3))
                if n:
                    route(n)
                if u.plus(-1):
                    second(u.plus(-1), 3)
                if u:
                    first(u, 1)
                    spread_gates(u, 1)
                if n:
                    tp_logits(n)
                if u:
                    second(u, 0)
                if u.plus(3):
                    attend(u.plus(3), 0)
                if u:
                    first(u, 2)
                    spread_gates(u, 2)
                    second(u, 1)
                if u.plus(3):
                    attend(u.plus(3), 1)
                if u:
                    first(u, 3)
                    spread_gates(u, 3)
                if u.plus(2):
                    tp_e(u.plus(2))
                if u:
                    second(u, 2)
                if n:
                    tp_gates(n)

            pe.wait_ge(w_ready, NU)
            pipeline(te, step_e, -3, 2, NU - 4)
            second(unit(NU - 1), 3)

        @block.vector
        def _(dve):
            ve = nc.vector
            TT = ve.tensor_tensor

            for rows in (bqk_r[:, :], bo_r[:, :, :], b2_hi[:, :], b2_lo[:, :], gT[:, :, :]):
                last = ve.memset(rows.bitcast(F32), 0.0)
            last.then_inc(zero_rows, 1)
            ve.memset(ones_r[:, :].bitcast(F32), 1.0)
            ve.memset(kv_acc[:, :, :, :], 0.0).then_inc(acc_zero, 1)

            def stats_of(u, x_ready, st, done, pooled):
                h = u.h
                x_ready()
                for t in range(2):
                    last = ve.bn_stats(stats[:, h, t, :], x_sb[:, u.tile(t), :])
                last.then_inc(st, 1)
                wait(dve, pooled, u.count(1, -1))
                wait_alone(dve, met_v, st, u.count(2, 1))
                for t in range(2):
                    last = ve.bn_aggr(mv[:, h, t, :], stats[:, h, t, :])
                last.then_inc(st, 1)
                wait(dve, st, u.count(2, 2))
                ve.tensor_scalar(neg_mean[:, h, :], mv[:, h, :, 0], -1.0, None, ALU.mult)
                ve.tensor_scalar(var_eps[:, h, :], mv[:, h, :, 1], LN_EPS, None, ALU.add).then_inc(done, 1)

            def stats_a(u):
                stats_of(u, lambda: dve.wait_ge(x_in[u.h], (u.it + 1) * 16), a_st, a_stats, a_rstd)

            u0 = unit(0)
            stats_a(u0)

            dve.wait_ge(c_exp_ready, 1)
            ve.tensor_scalar(c_den[:, :, :], c_exp[:, :, :], 1.0, None, ALU.add).then_inc(silu_step, 1)
            dve.wait_ge(silu_step, 1)
            ve.reciprocal(c_rec[:, :, :], c_den[:, :, :]).then_inc(silu_step, 1)
            dve.wait_ge(silu_step, 2)
            TT(c_silu[:, :, :], c_sb[:, :, :], c_rec[:, :, :], ALU.mult).then_inc(silu_step, 1)
            dve.wait_ge(silu_step, 3)
            for c in range(NC):
                last = ve.tensor_copy(c_rep[:, c, :, :],
                                      c_silu[:, c, :].rearrange("p (b o) -> p b o", o=1).to_broadcast([P, B, P]))
            last.then_inc(c_rep_ready, 1)

            dve.wait_ge(d_qkv, 16)
            for c in range(NC):
                ve.tensor_copy(wqkv_hi[:, c, :], wqkv_raw[:, c, :]).then_inc(qkv_step, 1)
            for c in range(NC):
                dve.wait_ge(qkv_step, c + 1)
                last = TT(wqkv_lo[:, c, :], wqkv_raw[:, c, :], wqkv_hi[:, c, :].bitcast(F32), ALU.subtract)
            last.then_inc(qkv_ready, 1)

            dve.wait_ge(d_small, 16 * N_SMALL)
            dve.wait_ge(zero_rows, 1)
            ve.tensor_copy(bqk_t[32:33, :], bqk_raw[32:33, :]).then_inc(bqk_step, 1)
            ve.tensor_copy(bqk_r[0:1, :], bqk_raw[0:1, :])
            dve.wait_ge(bqk_step, 1)
            TT(bqk_r[32:33, :], bqk_raw[32:33, :], bqk_t[32:33, :].bitcast(F32), ALU.subtract).then_inc(bqk_ready, 1)

            dve.wait_ge(modcol_done, 1)
            mc = bank[5][:, 0:4 * B].rearrange("p (k b) -> p k b", b=B)
            ve.tensor_copy(mod_col[:, 0:2, :], mc[:, 0:2, :])
            ve.tensor_scalar(mod_col[:, 2:4, :], mc[:, 2:4, :], 1.0, None, ALU.add).then_inc(modcol_ready, 1)
            stats_a(u0.plus(1))

            def mod_rows(b):
                dve.wait_ge(modrow_done, b + 1)
                ga, sb_ = (bank[6][:, k * E:(k + 1) * E] for k in range(2))
                cb, gb = (bank[7][:, k * E:(k + 1) * E] for k in range(2))
                ve.tensor_copy(mod_row[:, b, 1, :], sb_)
                ve.tensor_scalar(mod_row[:, b, 2, :], cb, 1.0, None, ALU.add)
                for i, (k, src) in enumerate(((0, ga), (3, gb))):
                    n = MODROW_STEPS * b + 4 * i
                    wait(dve, modrow_step, n)
                    ve.tensor_scalar(gate_sign[:, :], src, 0.0, 2.0, ALU.is_ge, ALU.mult).then_inc(modrow_step, 1)
                    wait(dve, modrow_step, n + 1)
                    ve.scalar_tensor_tensor(gate_abs[:, :], gate_sign[:, :], -1.0, src, ALU.add, ALU.mult)\
                        .then_inc(modrow_step, 1)
                    wait(dve, modrow_step, n + 2)
                    ve.tensor_scalar(gate_size[:, :], gate_abs[:, :], GATE_MIN, None, ALU.max)\
                        .then_inc(modrow_step, 1)
                    wait(dve, modrow_step, n + 3)
                    ve.scalar_tensor_tensor(mod_row[:, b, k, :], gate_sign[:, :], -1.0, gate_size[:, :],
                                            ALU.add, ALU.mult).then_inc(modrow_step, 1)

            def small_weights():
                dve.wait_ge(modrow_step, MODROW_STEPS * B)
                for row in (0, 32):
                    for b in range(B):
                        last = TT(bo_g[row:row + 1, b, :], bo_raw[row:row + 1, :], mod_row[row:row + 1, b, 0, :],
                                  ALU.mult)
                last.then_inc(small_step, 1)
                dve.wait_ge(small_step, 1)
                ve.tensor_copy(bo_t[32:33, :, :], bo_g[32:33, :, :])
                ve.tensor_copy(b2_hi[0:2 * NE, :], b2_raw[:, :])
                ve.tensor_copy(route_hi[:, :, :], route_raw[:, :, :]).then_inc(small_step, 1)
                dve.wait_ge(small_step, 2)
                ve.tensor_copy(bo_r[0:1, :, :], bo_g[0:1, :, :])
                TT(bo_r[32:33, :, :], bo_g[32:33, :, :], bo_t[32:33, :, :].bitcast(F32), ALU.subtract)
                TT(b2_lo[0:2 * NE, :], b2_raw[:, :], b2_hi[0:2 * NE, :].bitcast(F32), ALU.subtract)
                TT(route_lo[:, :, :], route_raw[:, :, :], route_hi[:, :, :].bitcast(F32), ALU.subtract)
                TT(cent_sq[:, :, :], route_raw[:, :, 0:NE], route_raw[:, :, 0:NE], ALU.mult).then_inc(small_ready, 1)

            def split_a(u):
                h = u.h
                wait(dve, a_hf, u.count(1, 1))
                wait(dve, a_v, u.count(1, -1))
                ve.tensor_copy(tr_hi[:, h, :, :], tr_f[:, h, :, :]).then_inc(a_hi, 1)

            def feature_map(u, t):
                h = u.h
                wait(dve, a_exp, u.count(2, t + 1))
                if t == 0:
                    wait(dve, a_kv, u.count(1, -1))
                    wait(dve, a_kst, u.count(2, -1))
                ve.scalar_tensor_tensor(q_sb[:, u.tile(t), :], bank[2 + t][:, 0:E], 1.0, e_sb[:, t, 0:E],
                                        ALU.add, ALU.max)
                ve.scalar_tensor_tensor(k_sb[:, h, t, :], bank[2 + t][:, E:2 * E], 1.0, e_sb[:, t, E:2 * E],
                                        ALU.add, ALU.max).then_inc(a_fm, 1)

            def add_kv(u):
                b = u.batch()
                wait(dve, a_kv, u.count(1, 1))
                wait(dve, a_acc, u.count(1, 0))
                acc = kv_acc[:, b, :, :].rearrange("p c n -> p (c n)")
                TT(acc, acc, bank[6 + u.h][:, 0:E], ALU.add).then_inc(a_acc, 1)

            def split_weights(u):
                i = u.count(1, 0)
                if isinstance(i, int):
                    dve.wait_ge(d_w, 48)
                src = w_raw[:, bass.ds(i, 1), :]
                hi = w_hi[:, bass.ds(i, 1), :]
                ve.tensor_copy(hi, src).then_inc(w_hi_done, 1)
                wait(dve, w_hi_done, u.count(1, 1))
                TT(w_lo[:, bass.ds(i, 1), :], src, hi.bitcast(F32), ALU.subtract).then_inc(w_ready, 1)

            def step_a(u):
                if u.plus(-2):
                    add_kv(u.plus(-2))
                split_weights(u)
                if u.plus(1):
                    split_a(u.plus(1))
                if not u.plus(1):
                    dve.wait_ge(w_ready, NU)
                feature_map(u, 0)
                feature_map(u, 1)
                if u.plus(3):
                    stats_a(u.plus(3))

            dve.wait_ge(const_ready, 1)
            ve.tensor_copy(sel[:, :, :], sel_f[:, :, :]).then_inc(sel_ready, 1)
            split_a(u0)
            stats_a(unit(2))
            mod_rows(0)
            dve.wait_ge(acc_zero, 1)
            step_a(u0)
            mod_rows(1)
            small_weights()
            pipeline(ve, step_a, 1, 2, NU - 4)
            add_kv(unit(NU - 2))
            add_kv(unit(NU - 1))

            dve.wait_ge(cent_done, 1)
            ve.tensor_scalar(cent_n2[:, :], bank[6][:, 0:NE], NORM_EPS2, None, ALU.max).then_inc(cent_n2_ready, 1)

            dve.wait_ge(f_ksum, 1)
            for b in range(B):
                ve.tensor_copy(ksum_row[:, b, :], bank[7][:, b * E:(b + 1) * E]).then_inc(f_ksrow, 1)
            dve.wait_ge(f_ksrow, B)
            dve.wait_ge(a_acc, NU)
            for b in range(B):
                if b:
                    dve.wait_ge(f_kvm, b)
                for c in range(NC):
                    last = ve.scalar_tensor_tensor(kv_b[:, c, :], ksum_row[:, b, c * P:(c + 1) * P],
                                                   bv_sb[:, c:c + 1], kv_acc[:, b, c, :], ALU.mult, ALU.add)
                last.then_inc(f_step, 1)
                dve.wait_ge(f_step, 3 * b + 1)
                for c in range(NC):
                    last = TT(kv_m[:, b, c, :], kv_b[:, c, :], head_mask[:, :], ALU.mult)
                last.then_inc(f_kvm, 1)
                dve.wait_ge(f_m, b + 1)
                for c in range(NC):
                    last = TT(m_f[:, b, c, :], bank[4 + b][:, c * E:(c + 1) * E], mod_row[:, b, 0, :], ALU.mult)
                last.then_inc(f_step, 1)
                dve.wait_ge(f_step, 3 * b + 2)
                ve.tensor_copy(m_hi[:, b, :, :], m_f[:, b, :, :]).then_inc(f_step, 1)
                dve.wait_ge(f_step, 3 * b + 3)
                TT(m_lo[:, b, :, :], m_f[:, b, :, :], m_hi[:, b, :, :].bitcast(F32), ALU.subtract)\
                    .then_inc(f_ready, 1)

            def denominators(u):
                wait(dve, o_prod, u.count(1, 1))
                wait(dve, o_qz, u.count(1, 0))
                ve.tensor_reduce(den[:, :, :].rearrange("p t h -> p (t h)"),
                                 prod[:, :, :].rearrange("p t (h d) -> p (t h) d", d=D),
                                 axis=AXX, op=ALU.add).then_inc(o_den, 1)
                wait(dve, o_den, u.count(2, 1))
                ve.tensor_scalar(den_e[:, :, :], den[:, :, :], DEN_EPS, None, ALU.add).then_inc(o_den, 1)
                wait(dve, o_den, u.count(2, 2))
                ve.reciprocal(z[:, :, :], den_e[:, :, :]).then_inc(o_z, 1)

            def lo_o(u):
                wait(dve, o_hi, u.count(1, 1))
                TT(qz_lo.rearrange("p c n -> p (c n)"), bank[0][:, :],
                   qz_hi.rearrange("p c n -> p (c n)").bitcast(F32), ALU.subtract).then_inc(o_lo, 1)

            def add_attention(u):
                wait(dve, o_y, u.count(2, 2))
                xt = x_sb[:, bass.ds(u.tile(0), 2), :]
                TT(xt, xt, bank[0][:, :].rearrange("p (t e) -> p t e", t=2), ALU.add).then_inc(o_x1, 1)

            def stats_e(u):
                def x_ready():
                    wait_alone(dve, met_v, o_x1, u.count(1, 1))
                stats_of(u, x_ready, e_st, e_stats, e_rstd)

            def modulate_e(u):
                h, b = u.h, u.batch()
                wait(dve, e_rstd, u.count(1, 1))
                wait(dve, e_tp, u.count(1, -1))
                wait(dve, e_sq, u.count(2, -2))
                for t in range(2):
                    ve.scalar_tensor_tensor(xc[:, t, :], x_sb[:, u.tile(t), :], mv[:, h, t, 0:1],
                                            mod_row[:, b, 2, :], ALU.subtract, ALU.mult).then_inc(e_xc, 1)
                for t in range(2):
                    wait(dve, e_xc, u.count(2, t + 1))
                    last = ve.scalar_tensor_tensor(nat[:, h, t, :], xc[:, t, :], rstd[:, h, t:t + 1],
                                                   mod_row[:, b, 1, :], ALU.mult, ALU.add)
                last.then_inc(e_h, 1)

            def clip_norm(u):
                wait(dve, e_sq, u.count(2, 2))
                wait(dve, e_rn, u.count(1, -1))
                ve.tensor_scalar(h_n2c[:, u.h, :], h_n2[:, u.h, :], NORM_EPS2, None, ALU.max).then_inc(e_n2, 1)

            def lo_e(u):
                h = u.h
                wait(dve, e_hi, u.count(1, 1))
                TT(tr_lo[:, h, :, :].rearrange("p c n -> p (c n)"), bank[0][:, :],
                   tr_hi[:, h, :, :].rearrange("p c n -> p (c n)").bitcast(F32), ALU.subtract).then_inc(e_lo, 1)

            def gate(u, p):
                s = p % 2
                wait(dve, e_gelu, u.count(NP, p + 1))
                wait(dve, e_gb, u.count(NP, p + 1))
                wait(dve, e_hlo, u.count(NP, p - 1))
                TT(hid_g[:, s, :, :].rearrange("p j n -> p (j n)"), hid[:, s, :, :].rearrange("p j n -> p (j n)"),
                   bank[4 + s][:, :], ALU.mult).then_inc(e_mul, 1)

            G = 8

            def gates_a(u):
                wait(dve, e_lgT, u.count(1, 1))
                wait(dve, e_rn, u.count(1, 1))
                lg = bank[1][:, 0:4 * NE].rearrange("p (t k) -> p t k", t=2)
                TT(cosw[:, :, :], lg[:, :, 0:NE],
                   cent_rn[:, :].rearrange("p (o e) -> p o e", o=1).to_broadcast([P, 2, NE]), ALU.mult)\
                    .then_inc(e_gstep, 1)
                wait(dve, e_gstep, u.count(G, 1))
                for t in range(2):
                    last = ve.scalar_tensor_tensor(logit[:, t, :], cosw[:, t, :], h_rn[:, u.h, t:t + 1],
                                                   lg[:, t, NE:2 * NE], ALU.mult, ALU.add)
                last.then_inc(e_gstep, 1)
                wait_alone(dve, met_v, e_gstep, u.count(G, 2))
                for t in range(2):
                    last = ve.max(top[:, t, :], logit[:, t, :])
                last.then_inc(e_gstep, 1)
                wait(dve, e_gstep, u.count(G, 3))
                TT(shifted[:, :, :], logit[:, :, :], top[:, :, 0:1].to_broadcast([P, 2, NE]), ALU.subtract)\
                    .then_inc(e_shift, 1)
                TT(chosen[:, :, :], logit[:, :, :], top[:, :, 1:2].to_broadcast([P, 2, NE]), ALU.is_ge)\
                    .then_inc(e_gstep, 1)

            def gates_b(u):
                wait(dve, e_gstep, u.count(G, 4))
                wait(dve, e_gexp, u.count(1, 1))
                TT(g_sel[:, :, :], g_exp[:, :, :], chosen[:, :, :], ALU.mult).then_inc(e_gstep, 1)
                wait(dve, e_gstep, u.count(G, 5))
                ve.tensor_reduce(g_sum[:, :], g_sel[:, :, :], axis=AXX, op=ALU.add).then_inc(e_gstep, 1)
                wait(dve, e_gstep, u.count(G, 6))
                ve.reciprocal(g_rec[:, :], g_sum[:, :]).then_inc(e_gstep, 1)
                wait(dve, e_gstep, u.count(G, 7))
                wait(dve, e_gTp, u.count(1, 0))
                rec = g_rec[:, :].rearrange("p (t o) -> p t o", o=1).to_broadcast([P, 2, NE])
                TT(g_f[:, :, :], g_sel[:, :, :], rec, ALU.mult)
                TT(g_hilo[:, :, 0:NE], g_sel[:, :, :], rec, ALU.mult).then_inc(e_gstep, 1)
                wait(dve, e_gstep, u.count(G, 8))
                TT(g_hilo[:, :, NE:2 * NE].bitcast(F32), g_f[:, :, :], g_hilo[:, :, 0:NE].bitcast(F32), ALU.subtract)\
                    .then_inc(e_gnat, 1)

            def scale_experts(u):
                b = u.batch()
                wait(dve, e_f2, u.count(NP, NP))
                wait(dve, e_y, u.count(1, 0))
                for t in range(2):
                    last = TT(y_g[:, t, :], bank[6 + t][:, 0:E], mod_row[:, b, 3, :], ALU.mult)
                last.then_inc(e_yg, 1)

            def step_e(u):
                n = u.plus(1)
                if n:
                    clip_norm(n)
                if u:
                    gate(u, 0)
                if u.plus(3):
                    lo_o(u.plus(3))
                if u.plus(-1):
                    scale_experts(u.plus(-1))
                if u.plus(4):
                    denominators(u.plus(4))
                if u:
                    gate(u, 1)
                if n:
                    gates_a(n)
                if u.plus(2):
                    modulate_e(u.plus(2))
                if u:
                    gate(u, 2)
                if u.plus(3):
                    add_attention(u.plus(3))
                if n:
                    gates_b(n)
                if u:
                    gate(u, 3)
                if u.plus(2):
                    lo_e(u.plus(2))
                if u.plus(3):
                    stats_e(u.plus(3))

            dve.wait_ge(cent_ready, 1)
            pipeline(ve, step_e, -4, 2, NU - 4)
            scale_experts(unit(NU - 1))


def kernel(**inputs):
    import numpy as np
    import concourse.bacc as bacc
    from concourse.bass_utils import run_bass_kernel_spmd

    a = {k.replace("L0_", ""): np.asarray(v) for k, v in inputs.items()}
    B, S, E = a["attn_x"].shape
    route = np.concatenate([a["ffn_centroids"].T, a["ffn_w_route"].T], axis=1)
    given = {
        "x": a["attn_x"].reshape(B * S, E),
        "wqkvT": np.concatenate([a["attn_Wq"].T, a["attn_Wk"].T, a["attn_Wv"].T], axis=1),
        "rows": np.concatenate([a["attn_bq"], a["attn_bk"], a["attn_bo"]]).reshape(1, 3 * E),
        "cols": np.concatenate([route[:P], route[P:], a["attn_bv"].reshape(2, P).T, a["ffn_b1"].T], axis=1),
        "woT": a["attn_Wo"].T,
        "w1": a["ffn_w1"],
        "w2": a["ffn_w2"],
        "b2": np.concatenate([a["ffn_b2"], a["ffn_b2"]]),
        "cT": a["c"].T,
        "wmod": a["wmod"],
    }
    nc = bacc.Bacc("TRN2", target_bir_lowering=False, num_devices=1)
    arrays, args = {}, []
    for name, value in given.items():
        value = np.ascontiguousarray(value)
        arrays[f"in_{name}"] = value
        args.append(nc.dram_tensor(f"in_{name}", value.shape, mybir.dt.from_np(value.dtype), kind="ExternalInput").ap())
    out = nc.dram_tensor("out_0", (B * S, E), F32, kind="ExternalOutput").ap()
    adaln_block(nc, *args, out)
    got = run_bass_kernel_spmd(nc, [arrays], core_ids=[0])
    return got.results[0]["out_0"].reshape(B, S, E)
```

```python
import math

import concourse.bass as bass
from concourse import mybir
from contextlib import ExitStack


F32 = mybir.dt.float32
F32R = mybir.dt.float32r
ALU = mybir.AluOpType
ACT = mybir.ActivationFunctionType
AXX = mybir.AxisListType.X

P = 128
LN_EPS = 1e-5
DEN_EPS = 1e-6
NORM_EPS2 = 1e-24
GATE_MIN = 0.25


class Unit:

    def __init__(self, it, h, n_units, per_batch):
        self.it, self.h, self.n_units, self.per_batch = it, h, n_units, per_batch

    def plus(self, d):
        k = self.h + d
        return Unit(self.it + k // 2 if k // 2 else self.it, k % 2, self.n_units, self.per_batch)

    def __bool__(self):
        return not isinstance(self.it, int) or 0 <= 2 * self.it + self.h < self.n_units

    def nth(self, i):
        return isinstance(self.it, int) and 2 * self.it + self.h == i

    def count(self, n=1, c=0):
        return self.it * (2 * n) + (self.h * n + c)

    def tile(self, t):
        return self.it * 4 + (2 * self.h + t)

    def batch(self):
        return self.it // (self.per_batch // 2)


def wait(eng, sem, value):
    if isinstance(value, int) and value <= 0:
        return
    eng.wait_ge(sem, value)


MODROW_STEPS = 4
N_SMALL = 5


def adaln_block(nc, x, wqkvT, rows, cols, woT, w1, w2, b2, cT, wmod, out):
    S, E = x.shape
    B = cT.shape[1]
    NE, _, HID = w1.shape
    NC = E // P
    NT = S // P
    NU = NT // 2
    UPB = NU // B
    D = 16
    NH = E // D
    assert NC == 2 and HID == P and NE == 8 and B == 2 and UPB % 2 == 0 and NU >= 8
    NP = NE // 2

    ctx = ExitStack()
    with ctx:
        def sb(name, shape, dt=F32):
            return ctx.enter_context(nc.sbuf_tensor(name, shape, dt))

        def sem(name):
            return ctx.enter_context(nc.semaphore(name))

        def unit(u):
            return Unit(u // 2, u % 2, NU, UPB)

        def pipeline(eng, step, start, loop_from, loop_to, stop=NU):
            for u in range(start, loop_from):
                step(unit(u))
            with eng.Fori(loop_from // 2, loop_to // 2) as it:
                for h in range(2):
                    step(Unit(it, h, NU, UPB))
            for u in range(loop_to, stop):
                step(unit(u))

        x_sb = sb("x_sb", [P, NT, E])
        q_sb = sb("q_sb", [P, NT, E])
        ident = sb("ident", [P, P])
        ones_r = sb("ones_r", [P, P], F32R)
        ones_f = ones_r[:, :].bitcast(F32)
        head_mask = sb("head_mask", [P, P])
        sel = sb("sel", [P, NE, P], F32R)
        minus_half = sb("minus_half", [P, NE])
        euler = sb("euler", [P, 2 * NE])

        c_sb = sb("c_sb", [P, NC, B])
        c_exp = sb("c_exp", [P, NC, B])
        c_den = sb("c_den", [P, NC, B])
        c_rec = sb("c_rec", [P, NC, B])
        c_silu = sb("c_silu", [P, NC, B])
        early = sb("early", [P, NC * 6 * E])
        wmod_sb = early[:, :].rearrange("p (c n) -> p c n", c=NC)
        prod, qz, m_f = (early[:, i * 2 * E:(i + 1) * 2 * E].rearrange("p (t e) -> p t e", t=2) for i in range(3))
        kv_b, kv_m = (early[:, (6 + i) * E:(7 + i) * E].rearrange("p (c n) -> p c n", c=NC) for i in range(2))
        mod_col = sb("mod_col", [P, 4, B])
        mod_row = sb("mod_row", [P, B, 4, E])

        wm_hi = sb("wm_hi", [P, NC * 3 * E], F32R)
        wm_lo = sb("wm_lo", [P, NC * 3 * E], F32R)
        wqkv_hi, wqkv_lo = (m[:, :].rearrange("p (c n) -> p c n", c=NC) for m in (wm_hi, wm_lo))
        wqkv_raw = q_sb[:, 0:NC * 3, :].rearrange("p (c k) e -> p c (k e)", c=NC)
        m_hi = sb("m_hi", [P, B, NC, E], F32R)
        m_lo = sb("m_lo", [P, B, NC, E], F32R)
        qz_hi = sb("qz_hi", [P, NC, E], F32R)
        qz_lo = sb("qz_lo", [P, NC, E], F32R)
        hid = sb("hid", [P, 2, 2, 2 * P])
        hid_g = sb("hid_g", [P, 2, 2, 2 * P])
        hid_hi = sb("hid_hi", [P, 2, 2, 2 * P], F32R)
        hid_lo = sb("hid_lo", [P, 2, 2, 2 * P], F32R)
        before = [m[:, :, :, :].rearrange("p s j n -> p (s j n)") for m in (hid, hid_g, hid_hi)]
        rows_raw, b2_raw = before[0][0:33, 0:3 * E], before[0][0:48, 3 * E:4 * E]
        bqk_raw, bo_raw = rows_raw[:, 0:2 * E], rows_raw[:, 2 * E:3 * E]
        c_rep = before[1][:, 2 * E:4 * E].rearrange("p (c b n) -> p c b n", c=NC, b=B)
        bqk_t = before[2][0:33, 0:2 * E]
        b2_t = before[2][0:48, 2 * E:3 * E]
        gate_sign, gate_abs, gate_size = ([q_sb[:, 8 + 2 * k + i, :] for i in range(2)] for k in range(3))
        bo_sb = q_sb[:, 14, :]
        bqk_r = sb("bqk_r", [P, 2 * E], F32R)
        cols_sb = sb("cols_sb", [P, NC * 2 * NE + NC + NE])
        route_raw = cols_sb[:, 0:NC * 2 * NE].rearrange("p (c n) -> p c n", c=NC)
        bv_sb = cols_sb[:, NC * 2 * NE:NC * 2 * NE + NC]
        b1_sb = cols_sb[:, NC * 2 * NE + NC:]
        wo_sb = sb("wo_sb", [P, NC, E])
        ga_bo = sb("ga_bo", [P, B, E])
        w_raw = q_sb[:, NT - 2 * NE:NT, :]
        w1_raw = w_raw[:, 0:NE, :].rearrange("p (c g) (k j) -> p c (g k) j", c=NC, k=E // HID)
        w2_raw = w_raw[:, NE:2 * NE, :]
        w_hi = sb("w_hi", [P, 2 * NE, E], F32R)
        w_lo = sb("w_lo", [P, 2 * NE, E], F32R)
        w1_hi, w1_lo = (m[:, 0:NE, :].rearrange("p (c g) (k j) -> p c (g k) j", c=NC, k=E // HID)
                        for m in (w_hi, w_lo))
        w2_hi, w2_lo = (m[:, NE:2 * NE, :] for m in (w_hi, w_lo))
        b2_r = sb("b2_r", [P, E], F32R)
        route_r = sb("route_r", [P, NC, 4 * NE], F32R)
        fold = sb("fold", [4 * NE, 2 * NE])
        cent_sq = sb("cent_sq", [P, NC, NE])
        cent_n2 = sb("cent_n2", [P, NE])
        cent_rn = sb("cent_rn", [P, NE])

        stats = sb("stats", [P, 2, 2, 6])
        mv = sb("mv", [P, 2, 2, 2])
        var_eps = sb("var_eps", [P, 2, 2])
        neg_mean = sb("neg_mean", [P, 2, 2])
        rstd = sb("rstd", [P, 2, 2])
        neg_mr = sb("neg_mr", [P, 2, 2])
        nat = sb("nat", [P, 2, 2, E])
        tr_f = sb("tr_f", [P, 2, NC, 2 * P])
        tr_hi = sb("tr_hi", [P, 2, NC, 2 * P], F32R)
        tr_lo = sb("tr_lo", [P, 2, NC, 2 * P], F32R)
        e_sb = sb("e_sb", [P, 2, 2 * E])
        sel_f = e_sb[:, :, :].rearrange("p t (e q) -> p (t e) q", q=P)
        k_sb = sb("k_sb", [P, 2, 2, E])
        xc, y_g = k_sb[:, 0, :, :], k_sb[:, 1, :, :]
        v_sb = sb("v_sb", [P, 2, 2, E])
        sq = v_sb[:, 0, 0, :]
        lg_t = v_sb[0:4 * NE, 1, 0, :]
        k_sum = sb("k_sum", [P, B, E])
        kv_acc = sb("kv_acc", [P, B, NC, P])
        ksum_row = sb("ksum_row", [P, B, E])
        den = sb("den", [P, 2, NH])
        den_e = sb("den_e", [P, 2, NH])
        z = sb("z", [P, 2, NH])
        h_n2 = sb("h_n2", [P, 2, 2])
        h_n2c = sb("h_n2c", [P, 2, 2])
        h_rn = sb("h_rn", [P, 2, 2])
        cosw = sb("cosw", [P, 2, NE])
        logit = sb("logit", [P, 2, NE])
        top = sb("top", [P, 2, 8])
        shifted = sb("shifted", [P, 2, NE])
        chosen = sb("chosen", [P, 2, NE])
        g_exp = sb("g_exp", [P, 2, NE])
        g_sel = sb("g_sel", [P, 2, NE])
        g_sum = sb("g_sum", [P, 2])
        g_rec = sb("g_rec", [P, 2])
        g_f = sb("g_f", [P, 2, NE])
        g_hilo = sb("g_hilo", [P, 2, 2, 4 * NE], F32R)
        gT = sb("gT", [P, 2, 2 * P], F32R)
        bank = [ctx.enter_context(nc.psum_tensor(f"bank{i}", [P, 512], F32)) for i in range(8)]
        chunks = "p (c n) -> p c n"

        d_c = sem("d_c"); d_wmod = [sem(f"d_wmod{k}") for k in range(3)]; d_qkv = sem("d_qkv")
        d_wo = sem("d_wo"); d_w = sem("d_w"); d_small = sem("d_small")
        x_in = [sem(f"x_in{h}") for h in range(2)]
        y_out = [sem(f"y_out{h}") for h in range(2)]
        const_step = sem("const_step"); const_ready = sem("const_ready")
        c_exp_ready = sem("c_exp_ready"); silu_step = sem("silu_step"); c_rep_ready = sem("c_rep_ready")
        modcol_done = sem("modcol_done"); modcol_ready = sem("modcol_ready")
        modrow_done = sem("modrow_done"); modrow_step = sem("modrow_step")
        qkv_step = sem("qkv_step"); qkv_ready = sem("qkv_ready")
        zero_rows = sem("zero_rows"); sel_ready = sem("sel_ready"); ones_ready = sem("ones_ready")
        cent_done = sem("cent_done"); cent_n2_ready = sem("cent_n2_ready"); cent_ready = sem("cent_ready")
        w_hi_done = sem("w_hi_done"); w_ready = sem("w_ready")
        small_step = sem("small_step")
        bo_ready = sem("bo_ready"); bo_done = sem("bo_done"); ga_bo_ready = sem("ga_bo_ready"); a_bo = sem("a_bo")
        small_ready = sem("small_ready"); bqk_step = sem("bqk_step"); bqk_ready = sem("bqk_ready")

        a_st = sem("a_st"); a_stats = sem("a_stats"); a_pow = sem("a_pow"); a_rstd = sem("a_rstd")
        a_xn = sem("a_xn"); a_tp = sem("a_tp"); a_hf = sem("a_hf"); a_hi = sem("a_hi"); a_lo = sem("a_lo")
        a_qk = sem("a_qk"); a_v = sem("a_v"); a_exp = sem("a_exp"); a_vs = sem("a_vs"); a_neg = sem("a_neg")
        a_fm = sem("a_fm"); a_kst = sem("a_kst"); a_kv = sem("a_kv"); a_acc = sem("a_acc")

        f_ksum = sem("f_ksum"); f_ksrow = sem("f_ksrow"); f_step = sem("f_step"); f_kvm = sem("f_kvm")
        f_m = sem("f_m"); f_m_read = sem("f_m_read"); f_ready = sem("f_ready")

        o_prod = sem("o_prod"); o_den = sem("o_den"); o_z = sem("o_z"); o_qz = sem("o_qz"); o_tp = sem("o_tp")
        o_hi = sem("o_hi"); o_lo = sem("o_lo"); o_y = sem("o_y"); o_x1 = sem("o_x1")

        e_st = sem("e_st"); e_stats = sem("e_stats"); e_rstd = sem("e_rstd"); e_xc = sem("e_xc")
        e_h = sem("e_h"); e_sq = sem("e_sq"); e_n2 = sem("e_n2"); e_rn = sem("e_rn")
        e_tp = sem("e_tp"); e_hi = sem("e_hi"); e_lo = sem("e_lo")
        e_route = sem("e_route"); e_lgs = sem("e_lgs"); e_lgT = sem("e_lgT"); e_gstep = sem("e_gstep")
        e_shift = sem("e_shift"); e_gexp = sem("e_gexp"); e_gnat = sem("e_gnat"); e_gTp = sem("e_gTp")
        e_gT = sem("e_gT")
        e_f1 = sem("e_f1"); e_gb = sem("e_gb"); e_gelu = sem("e_gelu"); e_mul = sem("e_mul")
        e_hhi = sem("e_hhi"); e_hlo = sem("e_hlo"); e_hlo_v = sem("e_hlo_v")
        e_f2 = sem("e_f2"); e_yg = sem("e_yg"); e_y = sem("e_y")

        last_f2 = sem("last_f2"); last_scaled = sem("last_scaled"); last_y = sem("last_y")

        met_v = sem("met_v"); met_g = sem("met_g"); met_t = sem("met_t")

        def wait_alone(eng, met, on, value):
            wait(eng, on, value)
            if not isinstance(value, int):
                eng.sem_inc(met, 1)

        def lo_made(u, p):
            if p < 0:
                u, p = u.plus(-1), p + NP
            if u.nth(NU - 1) or u.nth(NU - 2):
                return e_hlo_v, u.count(NP, p + 1) - NP * (NU - 2)
            return e_hlo, u.count(NP, p + 1)

        def of_batch(columns, b):
            return columns[:, b:b + 1] if isinstance(b, int) else columns[:, bass.ds(b, 1)]

        wmod_chunks = wmod.rearrange("(c p) n -> p c n", p=P)

        block = ctx.enter_context(nc.Block())

        @block.sync
        def _(sp):
            def load_x(it, h):
                t = it * 4 + 2 * h
                wait(sp, x_in[h], it * 16)
                sp.dma_start(x_sb[:, bass.ds(t, 2), :], x_tiles[:, bass.ds(t, 2), :]).then_inc(x_in[h], 16)

            x_tiles = x.rearrange("(t p) e -> p t e", p=P)
            out_tiles = out.rearrange("(t p) e -> p t e", p=P)
            small = [(rows_raw[0:1, :], rows), (rows_raw[32:33, :], rows), (cols_sb[:, :], cols),
                     (b2_raw[0:2 * NE, :], b2), (b2_raw[32:32 + 2 * NE, :], b2)]
            assert len(small) == N_SMALL
            load_x(0, 0)
            sp.dma_start(wmod_sb[:, :, 0:2 * E], wmod_chunks[:, :, 0:2 * E]).then_inc(d_wmod[0], 16)
            sp.dma_start(wqkv_raw[:, :, :], wqkvT.rearrange("(c p) n -> p c n", p=P)).then_inc(d_qkv, 16)
            load_x(0, 1)
            for to, of in small:
                sp.dma_start(to, of).then_inc(d_small, 16)
            load_x(1, 0)
            load_x(1, 1)
            sp.dma_start(w1_raw[:, 0, :, :], w1[:, 0:P, :].rearrange("e p j -> p e j")).then_inc(d_w, 16)
            sp.dma_start(w1_raw[:, 1, :, :], w1[:, P:2 * P, :].rearrange("e p j -> p e j")).then_inc(d_w, 16)
            sp.dma_start(w2_raw, w2.rearrange("e p d -> p e d")).then_inc(d_w, 16)
            sp.dma_start(wo_sb[:, :, :], woT.rearrange("(c p) n -> p c n", p=P)).then_inc(d_wo, 16)
            with sp.Fori(2, NU // 2) as it:
                for h in range(2):
                    load_x(it, h)

            def store(u):
                wait(sp, e_y, u.count(1, 1))
                sp.dma_start(out_tiles[:, bass.ds(u.tile(0), 2), :],
                             x_sb[:, bass.ds(u.tile(0), 2), :]).then_inc(y_out[u.h], 16)

            pipeline(sp, store, 0, 2, NU - 2, NU - 1)
            for t in range(2):
                sp.wait_ge(last_y, t + 1)
                sp.dma_start(out_tiles[:, NT - 2 + t, :], x_sb[:, NT - 2 + t, :]).then_inc(y_out[1], 16)
            sp.wait_ge(y_out[0], 16 * (NU // 2))
            sp.wait_ge(y_out[1], 16 * (NU // 2 + 1))

        @block.gpsimd
        def _(pool):
            gp = nc.gpsimd
            gp.memset(ident[:, :], 0.0).then_inc(const_step, 1)
            gp.memset(sel_f[:, :, :], 0.0).then_inc(const_step, 1)
            gp.memset(head_mask[:, :], 1.0).then_inc(const_step, 1)
            gp.memset(minus_half[:, :], -0.5)
            gp.memset(euler[:, :], math.e)
            pool.wait_ge(const_step, 3)
            gp.affine_select(out=ident[:, :], in_=ident[:, :], compare_op=ALU.not_equal, fill=1.0,
                             base=0, pattern=[[-1, P]], channel_multiplier=1)
            gp.affine_select(out=sel_f[:, :, :], in_=sel_f[:, :, :], compare_op=ALU.not_equal, fill=1.0,
                             base=0, pattern=[[-1, NE], [0, P]], channel_multiplier=1).then_inc(const_step, 1)
            heads = head_mask[:, :].rearrange("p (h d) -> p h d", d=D)
            gp.affine_select(out=heads, in_=heads, compare_op=ALU.is_ge, fill=0.0,
                             base=0, pattern=[[-D, P // D], [0, D]], channel_multiplier=1).then_inc(const_step, 1)
            pool.wait_ge(const_step, 5)
            gp.affine_select(out=sel_f[:, :, :], in_=sel_f[:, :, :], compare_op=ALU.not_equal, fill=1.0,
                             base=-NE, pattern=[[-1, NE], [0, P]], channel_multiplier=1)
            gp.affine_select(out=heads, in_=heads, compare_op=ALU.is_ge, fill=0.0,
                             base=D - 1, pattern=[[D, P // D], [0, D]], channel_multiplier=-1)\
              .then_inc(const_ready, 1)
            gp.memset(k_sum[:, :, :], 0.0).then_inc(a_kst, 1)

            def rstd_a(u):
                h = u.h
                wait(pool, a_stats, u.count(1, 1))
                wait(pool, a_xn, u.count(1, -1))
                gp.tensor_tensor(rstd[:, h, :], var_eps[:, h, :], minus_half[:, 0:2], ALU.pow).then_inc(a_pow, 1)
                wait(pool, a_pow, u.count(1, 1))
                gp.tensor_tensor(neg_mr[:, h, :], neg_mean[:, h, :], rstd[:, h, :], ALU.mult).then_inc(a_rstd, 1)

            def split_lo(u):
                h = u.h
                wait(pool, a_hi, u.count(1, 1))
                wait(pool, a_v, u.count(1, -1))
                gp.tensor_tensor(tr_lo[:, h, :, :], tr_f[:, h, :, :], tr_hi[:, h, :, :].bitcast(F32), ALU.subtract)\
                  .then_inc(a_lo, 1)

            def add_ksum(u):
                b = u.batch()
                for t in range(2):
                    wait(pool, a_fm, u.count(2, t + 1))
                    wait_alone(pool, met_g, a_kst, u.count(2, t + 1))
                    add = gp.tensor_tensor(k_sum[:, b, :], k_sum[:, b, :], k_sb[:, u.h, t, :], ALU.add)
                    add.then_inc(a_kst, 1)

            def add_bo(u):
                wait_alone(pool, met_g, a_xn, u.count(1, 1))
                xt = x_sb[:, bass.ds(u.tile(0), 2), :]
                gp.tensor_tensor(xt, xt, ga_bo[:, bass.ds(u.batch(), 1), :].to_broadcast([P, 2, E]), ALU.add)\
                  .then_inc(a_bo, 1)

            def step_a(u):
                if u.plus(2):
                    rstd_a(u.plus(2))
                if u.plus(1):
                    split_lo(u.plus(1))
                if u.plus(-1):
                    add_ksum(u.plus(-1))
                if u.nth(2):
                    pool.wait_ge(ga_bo_ready, B)
                if u.plus(-2) and not u.plus(-2).nth(NU - 4) and not u.plus(-2).nth(NU - 3):
                    add_bo(u.plus(-2))

            u0 = unit(0)
            rstd_a(u0)
            rstd_a(u0.plus(1))
            split_lo(u0)

            def make_prod(u):
                if u.nth(0):
                    pool.wait_ge(f_ksrow, 1)
                if u.nth(5):
                    pool.wait_ge(f_ksrow, B)
                wait_alone(pool, met_g, o_z, u.count(1, 0))
                gp.tensor_tensor(prod[:, :, :], q_sb[:, bass.ds(u.tile(0), 2), :],
                                 ksum_row[:, bass.ds(u.batch(), 1), :].to_broadcast([P, 2, E]),
                                 ALU.mult).then_inc(o_prod, 1)

            def make_qz(u):
                wait(pool, o_z, u.count(1, 1))
                wait_alone(pool, met_g, o_tp, u.count(1, 0))
                q4 = q_sb[:, bass.ds(u.tile(0), 2), :].rearrange("p t (h d) -> p (t h) d", d=D)
                n4 = qz[:, :, :].rearrange("p t (h d) -> p (t h) d", d=D)
                z4 = z[:, :, :].rearrange("p t (h o) -> p (t h) o", o=1).to_broadcast([P, 2 * NH, D])
                gp.tensor_tensor(n4, q4, z4, ALU.mult).then_inc(o_qz, 1)

            def rstd_e(u):
                wait(pool, e_stats, u.count(1, 1))
                wait(pool, e_h, u.count(1, -1))
                if u.nth(0):
                    pool.wait_ge(a_xn, NU)
                gp.tensor_tensor(rstd[:, u.h, :], var_eps[:, u.h, :], minus_half[:, 0:2], ALU.pow)\
                  .then_inc(e_rstd, 1)

            def norm_e(u):
                wait(pool, e_n2, u.count(1, 1))
                wait(pool, e_gnat, u.count(1, -1))
                gp.tensor_tensor(h_rn[:, u.h, :], h_n2c[:, u.h, :], minus_half[:, 0:2], ALU.pow)\
                  .then_inc(e_rn, 1)

            def lo_e(u, p):
                if u.nth(NU - 1) or u.nth(NU - 2):
                    return
                s = p % 2
                wait(pool, e_hhi, u.count(NP, p + 1))
                wait(pool, e_f2, u.count(NP, p - 1))
                gp.tensor_tensor(hid_lo[:, s, :, :], hid_g[:, s, :, :], hid_hi[:, s, :, :].bitcast(F32),
                                 ALU.subtract).then_inc(e_hlo, 1)

            def exp_gates(u):
                wait_alone(pool, met_g, e_shift, u.count(1, 1))
                gp.tensor_tensor(g_exp[:, :, :].rearrange("p t e -> p (t e)"), euler[:, :],
                                 shifted[:, :, :].rearrange("p t e -> p (t e)"), ALU.pow).then_inc(e_gexp, 1)

            def add_experts(u):
                wait_alone(pool, met_g, e_yg, u.count(1, 1))
                xt = x_sb[:, bass.ds(u.tile(0), 2), :]
                gp.tensor_tensor(xt, xt, y_g[:, :, :], ALU.add).then_inc(e_y, 1)

            def step_e(u):
                if u.plus(1):
                    norm_e(u.plus(1))
                if u.plus(4) and not u.nth(0):
                    make_prod(u.plus(4))
                if u:
                    lo_e(u, 0)
                if u.nth(0):
                    make_prod(u.plus(4))
                if u.plus(-1):
                    add_experts(u.plus(-1))
                if u:
                    lo_e(u, 1)
                if u.plus(1):
                    exp_gates(u.plus(1))
                if u:
                    lo_e(u, 2)
                if u.plus(4):
                    make_qz(u.plus(4))
                if u.nth(-2):
                    add_bo(unit(NU - 4))
                if u.nth(-1):
                    for j in (3, 2, 1):
                        add_bo(unit(NU - j))
                if u:
                    lo_e(u, 3)
                if u.plus(3):
                    rstd_e(u.plus(3))

            pipeline(gp, step_a, 0, 2, NU - 4, NU - 2)
            make_prod(u0)
            pool.wait_ge(cent_n2_ready, 1)
            gp.tensor_tensor(cent_rn[:, :], cent_n2[:, :], minus_half[:, :], ALU.pow).then_inc(cent_ready, 1)
            step_a(unit(NU - 2))
            make_qz(u0)
            make_prod(unit(1))
            make_qz(unit(1))
            step_a(unit(NU - 1))
            rstd_e(u0)
            add_ksum(unit(NU - 1))
            step_e(unit(-2))
            step_e(unit(-1))
            pipeline(gp, step_e, 0, 2, NU - 4)

        @block.scalar
        def _(act):
            ac = nc.scalar
            act.dma_start(c_sb[:, :, :], cT.rearrange("(c p) b -> p c b", p=P)).then_inc(d_c, 16)
            act.wait_ge(d_c, 16)
            ac.activation(c_exp[:, :, :], c_sb[:, :, :], ACT.Exp, scale=-1.0).then_inc(c_exp_ready, 1)
            for k in range(1, 3):
                cols_k = slice(k * 2 * E, (k + 1) * 2 * E)
                act.dma_start(wmod_sb[:, :, cols_k], wmod_chunks[:, :, cols_k]).then_inc(d_wmod[k], 16)

            def normalise(u):
                wait(act, a_rstd, u.count(1, 1))
                wait(act, a_tp, u.count(1, -1))
                for t in range(2):
                    last = ac.activation(nat[:, u.h, t, :], x_sb[:, u.tile(t), :], ACT.Identity,
                                         bias=neg_mr[:, u.h, t:t + 1], scale=rstd[:, u.h, t:t + 1])
                last.then_inc(a_xn, 1)

            def modulate(u, b):
                wait(act, a_tp, u.count(1, 1))
                wait(act, a_lo, u.count(1, -1))
                tp = bank[u.h][:, :].rearrange(chunks, c=NC)
                for c in range(NC):
                    last = ac.activation(tr_f[:, u.h, c, :], tp[:, c, :], ACT.Identity,
                                         bias=of_batch(mod_col[:, c, :], b), scale=of_batch(mod_col[:, 2 + c, :], b))
                last.then_inc(a_hf, 1)

            def negative_part(u, t):
                wait(act, a_qk, u.count(2, t + 1))
                if u.nth(0):
                    act.wait_ge(sel_ready, 1)
                ac.activation(e_sb[:, t, :], bank[2 + t][:, :], ACT.Relu, scale=-1.0).then_inc(a_neg, 1)

            def exp_qk(u, t):
                wait(act, a_neg, u.count(2, t + 1))
                ac.activation(e_sb[:, t, :], e_sb[:, t, :], ACT.Exp, scale=-1.0).then_inc(a_exp, 1)

            def keep_v(u):
                wait(act, a_v, u.count(1, 1))
                wait(act, a_kv, u.count(1, -1))
                ac.activation(v_sb[:, u.h, :, :].rearrange("p t e -> p (t e)"), bank[4 + u.h][:, :], ACT.Copy)\
                  .then_inc(a_vs, 1)

            def step_a(u):
                negative_part(u, 0)
                if u.plus(1):
                    modulate(u.plus(1), u.plus(1).batch())
                exp_qk(u, 0)
                negative_part(u, 1)
                exp_qk(u, 1)
                if u.plus(2):
                    normalise(u.plus(2))
                if not u.nth(NU - 1):
                    keep_v(u)

            u0 = unit(0)
            normalise(u0)
            act.wait_ge(modcol_ready, 1)
            modulate(u0, 0)
            normalise(u0.plus(1))

            def hi_o(u):
                wait(act, o_tp, u.count(1, 1))
                wait(act, o_y, u.count(2, 0))
                ac.activation(qz_hi[:, :, :].rearrange("p c n -> p (c n)"), bank[0][:, :], ACT.Copy).then_inc(o_hi, 1)

            def square(u):
                wait(act, e_h, u.count(1, 1))
                wait(act, e_n2, u.count(1, -1))
                for t in range(2):
                    wait(act, e_sq, u.count(2, t))
                    ac.activation(sq[:, :], nat[:, u.h, t, :], ACT.Square,
                                  accum_out=h_n2[:, u.h, t:t + 1]).then_inc(e_sq, 1)

            def hi_e(u):
                wait(act, e_tp, u.count(1, 1))
                wait(act, e_f1, u.count(NP, -NP))
                ac.activation(tr_hi[:, u.h, :, :].rearrange("p c n -> p (c n)"), bank[0][:, :], ACT.Copy)\
                  .then_inc(e_hi, 1)

            def keep_logits(u):
                wait(act, e_route, u.count(1, 1))
                ac.activation(lg_t[:, :], bank[1][0:4 * NE, 0:2 * P], ACT.Copy).then_inc(e_lgs, 1)

            def keep_gates(u):
                wait(act, e_gTp, u.count(1, 1))
                wait(act, e_gb, u.count(NP, -NP))
                ac.activation(gT[0:8 * NE, u.h, :], bank[1][0:8 * NE, 0:2 * P], ACT.Copy).then_inc(e_gT, 1)

            def gelu(u, p):
                s = p % 2
                wait(act, e_f1, u.count(NP, p + 1))
                wait(act, e_mul, u.count(NP, p - 1))
                for j in range(2):
                    e = 2 * p + j
                    last = ac.activation(hid[:, s, j, :], bank[2 + s][:, 2 * P * j:2 * P * (j + 1)], ACT.Gelu,
                                         bias=b1_sb[:, e:e + 1])
                last.then_inc(e_gelu, 1)

            def hi_hid(u, p):
                s = p % 2
                wait(act, e_mul, u.count(NP, p + 1))
                wait(act, e_f2, u.count(NP, p - 1))
                ac.activation(hid_hi[:, s, :, :].rearrange("p j n -> p (j n)"),
                              hid_g[:, s, :, :].rearrange("p j n -> p (j n)"), ACT.Copy).then_inc(e_hhi, 1)

            def step_e(u):
                n = u.plus(1)
                if u:
                    gelu(u, 0)
                if u.nth(-1):
                    keep_logits(n)
                if u.plus(3):
                    hi_o(u.plus(3))
                if u:
                    hi_hid(u, 0)
                    if n:
                        keep_logits(n)
                if u:
                    gelu(u, 1)
                    hi_hid(u, 1)
                    gelu(u, 2)
                    hi_hid(u, 2)
                if u.plus(2):
                    square(u.plus(2))
                if u:
                    gelu(u, 3)
                if u.plus(2):
                    hi_e(u.plus(2))
                if u:
                    hi_hid(u, 3)
                if n:
                    keep_gates(n)

            pipeline(ac, step_a, 0, 2, NU - 4, NU - 1)
            hi_o(u0)
            step_a(unit(NU - 1))
            hi_o(unit(1))
            keep_v(unit(NU - 1))
            square(u0)
            hi_e(u0)
            pipeline(ac, step_e, -1, 2, NU - 4)

        @block.tensor
        def _(pe):
            te = nc.tensor

            def mm3(out_ap, l_hi, l_lo, r_hi, r_lo, start, stop):
                te.matmul(out_ap, l_hi, r_hi, start=start, stop=False)
                te.matmul(out_ap, l_hi, r_lo, start=False, stop=False)
                return te.matmul(out_ap, l_lo, r_hi, start=False, stop=stop)

            def transposes(of, to):
                dst = to[:, :].rearrange(chunks, c=NC)
                for c in range(NC):
                    for t in range(2):
                        last = te.transpose(dst[:, c, t * P:(t + 1) * P], of[:, t, c * P:(c + 1) * P],
                                            ident[:, :])
                return last

            def tp_a(u):
                wait(pe, a_xn, u.count(1, 1))
                wait(pe, a_hf, u.count(1, -1))
                if u.nth(NU - 2):
                    pe.wait_ge(f_ksrow, 1)
                    pe.wait_ge(cent_n2_ready, 1)
                if u.nth(NU - 1):
                    pe.wait_ge(f_m_read, 1)
                transposes(nat[:, u.h, :, :], bank[u.h]).then_inc(a_tp, 1)

            def qk(u, t):
                h = u.h
                if t == 0:
                    wait(pe, a_lo, u.count(1, 1))
                tok = slice(t * P, (t + 1) * P)
                wait(pe, a_fm, u.count(2, t - 1))
                te.matmul(bank[2 + t][:, :], ones_r[:, :], bqk_r[:, :], start=True, stop=False)
                for c in range(NC):
                    last = mm3(bank[2 + t][:, :], tr_hi[:, h, c, tok], tr_lo[:, h, c, tok],
                               wqkv_hi[:, c, 0:2 * E], wqkv_lo[:, c, 0:2 * E], False, c == NC - 1)
                last.then_inc(a_qk, 1)

            def v(u):
                h = u.h
                wait(pe, a_vs, u.count(1, -1))
                if u.nth(0):
                    pe.wait_ge(bo_ready, 1)
                for t in range(2):
                    tok = slice(t * P, (t + 1) * P)
                    for c in range(NC):
                        last = mm3(bank[4 + h][:, t * E:(t + 1) * E], tr_hi[:, h, c, tok], tr_lo[:, h, c, tok],
                                   wqkv_hi[:, c, 2 * E:3 * E], wqkv_lo[:, c, 2 * E:3 * E], c == 0, c == NC - 1)
                last.then_inc(a_v, 1)

            def kv(u):
                h = u.h
                wait(pe, a_fm, u.count(2, 2))
                wait(pe, a_vs, u.count(1, 1))
                wait(pe, a_acc, u.count(1, 0))
                if u.nth(0):
                    pe.wait_ge(modrow_step, MODROW_STEPS * B)
                for c in range(NC):
                    f = slice(c * P, (c + 1) * P)
                    for t in range(2):
                        last = te.matmul(bank[6 + h][:, f], v_sb[:, h, t, f], k_sb[:, h, t, f],
                                         start=(t == 0), stop=(t == 1))
                last.then_inc(a_kv, 1)

            def step_a(u):
                qk(u, 0)
                if u.plus(1):
                    tp_a(u.plus(1))
                qk(u, 1)
                v(u)
                if u.plus(-1):
                    kv(u.plus(-1))

            u0 = unit(0)
            pe.wait_ge(d_wmod[0], 16)
            pe.wait_ge(c_rep_ready, 1)
            for k in range(4):
                for c in range(NC):
                    last = te.matmul(bank[5][:, k * B:(k + 1) * B], wmod_sb[:, c, k * P:(k + 1) * P],
                                     c_silu[:, c, :], start=(c == 0), stop=(c == NC - 1))
            last.then_inc(modcol_done, 1)
            pe.wait_ge(const_ready, 1)
            tp_a(u0)

            def mod_rows(b):
                wait(pe, modrow_step, MODROW_STEPS * b)
                for k in range(2):
                    pe.wait_ge(d_wmod[1 + k], 16)
                    for c in range(NC):
                        last = te.matmul(bank[6 + k][:, :], c_rep[:, c, b, :],
                                         wmod_sb[:, c, 2 * E * (k + 1):2 * E * (k + 2)],
                                         start=(c == 0), stop=(c == NC - 1))
                last.then_inc(modrow_done, 1)

            mod_rows(0)
            pe.wait_ge(d_small, 16 * N_SMALL)
            pe.wait_ge(ones_ready, 1)
            te.matmul(bank[4][:, 0:E], ones_f[0:1, :], bo_raw[0:1, :], start=True, stop=True).then_inc(bo_done, 1)
            pe.wait_ge(qkv_ready, 1)
            pe.wait_ge(bqk_ready, 1)
            step_a(u0)
            mod_rows(1)
            pipeline(te, step_a, 1, 2, NU - 4, NU - 3)

            def sum_k(b, to):
                pe.wait_ge(a_kst, 2 * UPB * (b + 1) + 1)
                te.matmul(to, ones_f, k_sum[:, b, :], start=True, stop=True).then_inc(f_ksum, 1)

            def make_m(b, to):
                pe.wait_ge(f_kvm, b + 1)
                for c in range(NC):
                    last = te.matmul(to[:, c * E:(c + 1) * E], kv_m[:, c, :], wo_sb[:, c, :], start=True, stop=True)
                last.then_inc(f_m, 1)

            pe.wait_ge(small_ready, 1)
            pe.wait_ge(a_hf, NU - 3)
            for c in range(NC):
                last = te.matmul(bank[0][:, E:E + NE], ones_f, cent_sq[:, c, :], start=(c == 0), stop=(c == NC - 1))
            last.then_inc(cent_done, 1)
            sum_k(0, bank[0][:, 0:E])
            step_a(unit(NU - 3))
            pe.wait_ge(d_wo, 16)
            pe.wait_ge(a_hf, NU - 2)
            make_m(0, bank[1])

            def tp_o(u):
                wait(pe, o_qz, u.count(1, 1))
                wait(pe, o_x1, u.count(1, 0))
                wait(pe, e_lo, u.count(1, -1))
                transposes(qz[:, :, :], bank[0]).then_inc(o_tp, 1)

            def attend(u, t):
                b = u.batch()
                wait(pe, o_lo, u.count(1, 1))
                tok = slice(t * P, (t + 1) * P)
                to = bank[0][:, t * E:(t + 1) * E]
                for c in range(NC):
                    last = mm3(to, qz_hi[:, c, tok], qz_lo[:, c, tok], m_hi[:, b, c, :], m_lo[:, b, c, :],
                               c == 0, c == NC - 1)
                last.then_inc(o_y, 1)

            def tp_e(u):
                wait(pe, e_h, u.count(1, 1))
                if u.plus(1):
                    wait(pe, o_x1, u.count(1, 2))
                transposes(nat[:, u.h, :, :], bank[0]).then_inc(e_tp, 1)

            def route(u):
                h = u.h
                wait(pe, e_lo, u.count(1, 1))
                wait(pe, e_gT, u.count(1, 0))
                for c in range(NC):
                    for k, part in enumerate((tr_hi, tr_lo)):
                        last = te.matmul(bank[1][0:4 * NE, 0:2 * P], route_r[:, c, :], part[:, h, c, :],
                                         start=(c == 0 and k == 0), stop=(c == NC - 1 and k == 1))
                last.then_inc(e_route, 1)

            def tp_logits(u):
                wait_alone(pe, met_t, e_lgs, u.count(1, 1))
                for t in range(2):
                    last = te.matmul(bank[1][:, t * 2 * NE:(t + 1) * 2 * NE], lg_t[:, t * P:(t + 1) * P],
                                     fold[:, :], start=True, stop=True)
                last.then_inc(e_lgT, 1)

            def tp_gates(u):
                wait_alone(pe, met_t, e_gnat, u.count(1, 1))
                for t in range(2):
                    last = te.transpose(bank[1][0:8 * NE, t * P:(t + 1) * P],
                                        g_hilo[:, t, :, :].rearrange("p d k -> p (d k)").bitcast(F32),
                                        ident[:, :])
                last.then_inc(e_gTp, 1)

            def first(u, p):
                h, s = u.h, p % 2
                wait(pe, e_gelu, u.count(NP, p - 1))
                for j in range(2):
                    e = 2 * p + j
                    to = bank[2 + s][:, 2 * P * j:2 * P * (j + 1)]
                    for c in range(NC):
                        last = mm3(to, w1_hi[:, c, e, :], w1_lo[:, c, e, :], tr_hi[:, h, c, :], tr_lo[:, h, c, :],
                                   c == 0, c == NC - 1)
                last.then_inc(e_f1, 1)

            def spread_gates(u, p):
                s = p % 2
                if p == 0:
                    wait(pe, e_gT, u.count(1, 1))
                wait(pe, e_mul, u.count(NP, p - 1))
                for j in range(2):
                    last = te.matmul(bank[4 + s][:, 2 * P * j:2 * P * (j + 1)], sel[:, 2 * p + j, :], gT[:, u.h, :],
                                     start=True, stop=True)
                last.then_inc(e_gb, 1)

            def second(u, p):
                s = p % 2
                wait(pe, *lo_made(u, p))
                if u.nth(0) and p == 0:
                    pe.wait_ge(f_ready, B)
                if p == 0:
                    wait(pe, e_yg, u.count(1, 0))
                for t in range(2):
                    tok = slice(t * P, (t + 1) * P)
                    to = bank[6 + t][:, 0:E]
                    if p == 0:
                        te.matmul(to, gT[:, u.h, tok], b2_r[:, :], start=True, stop=False)
                    for j in range(2):
                        e = 2 * p + j
                        last = mm3(to, hid_hi[:, s, j, tok], hid_lo[:, s, j, tok], w2_hi[:, e, :],
                                   w2_lo[:, e, :], False, p == NP - 1 and j == 1)
                last.then_inc(e_f2, 1)

            def second_at_end():
                p, s = NP - 1, (NP - 1) % 2
                pe.wait_ge(e_hhi, NU * NP)
                for t in range(2):
                    for j in range(2):
                        for w2_part in (w2_hi, w2_lo):
                            te.matmul(bank[6 + t][:, 0:E], hid_hi[:, s, j, t * P:(t + 1) * P],
                                      w2_part[:, 2 * p + j, :], start=False, stop=False)
                wait(pe, *lo_made(unit(NU - 1), p))
                for t in range(2):
                    for j in range(2):
                        last = te.matmul(bank[6 + t][:, 0:E], hid_lo[:, s, j, t * P:(t + 1) * P],
                                         w2_hi[:, 2 * p + j, :], start=False, stop=(j == 1))
                    last.then_inc(last_f2, 1)

            def step_e(u):
                n = u.plus(1)
                if u:
                    if not u.nth(0):
                        first(u, 0)
                    spread_gates(u, 0)
                if u.nth(-1):
                    route(n)
                    tp_o(u.plus(3))
                else:
                    if u.plus(3):
                        tp_o(u.plus(3))
                    if n:
                        route(n)
                if u.plus(-1):
                    second(u.plus(-1), 3)
                if u:
                    first(u, 1)
                    spread_gates(u, 1)
                if n:
                    tp_logits(n)
                if u:
                    second(u, 0)
                if u.plus(3):
                    attend(u.plus(3), 0)
                if u:
                    first(u, 2)
                    spread_gates(u, 2)
                    second(u, 1)
                if u.plus(3):
                    attend(u.plus(3), 1)
                if u:
                    first(u, 3)
                    spread_gates(u, 3)
                if u.nth(-1):
                    make_m(1, bank[7])
                    first(n, 0)
                if u.plus(2):
                    tp_e(u.plus(2))
                if u:
                    second(u, 2)
                if n:
                    tp_gates(n)

            step_a(unit(NU - 2))
            qk(unit(NU - 1), 0)
            tp_o(u0)
            qk(unit(NU - 1), 1)
            pe.wait_ge(f_ready, 1)
            attend(u0, 0)
            attend(u0, 1)
            kv(unit(NU - 2))
            tp_o(unit(1))
            v(unit(NU - 1))
            attend(unit(1), 0)
            attend(unit(1), 1)
            kv(unit(NU - 1))
            sum_k(1, bank[5][:, 0:E])
            tp_e(u0)
            pe.wait_ge(w_ready, NU)
            step_e(unit(-1))
            pipeline(te, step_e, 0, 2, NU - 4)
            second_at_end()

        @block.vector
        def _(dve):
            ve = nc.vector
            TT = ve.tensor_tensor

            for rows in (bqk_r[:, :], b2_r[:, :], gT[:, :, :], g_hilo[:, :, :, :]):
                last = ve.memset(rows.bitcast(F32), 0.0)
            last.then_inc(zero_rows, 1)
            ve.memset(ones_r[:, :].bitcast(F32), 1.0).then_inc(ones_ready, 1)
            ve.memset(kv_acc[:, :, :, :], 0.0).then_inc(a_acc, 1)

            def stats_of(u, x_ready, st, done, pooled):
                h = u.h
                x_ready()
                for t in range(2):
                    last = ve.bn_stats(stats[:, h, t, :], x_sb[:, u.tile(t), :])
                last.then_inc(st, 1)
                wait(dve, pooled, u.count(1, -1))
                wait_alone(dve, met_v, st, u.count(2, 1))
                for t in range(2):
                    last = ve.bn_aggr(mv[:, h, t, :], stats[:, h, t, :])
                last.then_inc(st, 1)
                wait(dve, st, u.count(2, 2))
                ve.tensor_scalar(neg_mean[:, h, :], mv[:, h, :, 0], -1.0, None, ALU.mult)
                ve.tensor_scalar(var_eps[:, h, :], mv[:, h, :, 1], LN_EPS, None, ALU.add).then_inc(done, 1)

            def stats_a(u):
                stats_of(u, lambda: dve.wait_ge(x_in[u.h], (u.it + 1) * 16), a_st, a_stats, a_rstd)

            u0 = unit(0)
            stats_a(u0)

            dve.wait_ge(c_exp_ready, 1)
            ve.tensor_scalar(c_den[:, :, :], c_exp[:, :, :], 1.0, None, ALU.add).then_inc(silu_step, 1)
            dve.wait_ge(silu_step, 1)
            ve.reciprocal(c_rec[:, :, :], c_den[:, :, :]).then_inc(silu_step, 1)
            dve.wait_ge(silu_step, 2)
            TT(c_silu[:, :, :], c_sb[:, :, :], c_rec[:, :, :], ALU.mult).then_inc(silu_step, 1)
            dve.wait_ge(silu_step, 3)
            for c in range(NC):
                last = ve.tensor_copy(c_rep[:, c, :, :],
                                      c_silu[:, c, :].rearrange("p (b o) -> p b o", o=1).to_broadcast([P, B, P]))
            last.then_inc(c_rep_ready, 1)

            stats_a(u0.plus(1))
            dve.wait_ge(const_ready, 1)
            ve.tensor_copy(sel[:, :, :], sel_f[:, :, :]).then_inc(sel_ready, 1)
            dve.wait_ge(d_qkv, 16)
            for c in range(NC):
                ve.tensor_copy(wqkv_hi[:, c, :], wqkv_raw[:, c, :]).then_inc(qkv_step, 1)

            dve.wait_ge(modcol_done, 1)
            mc = bank[5][:, 0:4 * B].rearrange("p (k b) -> p k b", b=B)
            ve.tensor_copy(mod_col[:, 0:2, :], mc[:, 0:2, :])
            ve.tensor_scalar(mod_col[:, 2:4, :], mc[:, 2:4, :], 1.0, None, ALU.add).then_inc(modcol_ready, 1)

            def split_a(u):
                h = u.h
                wait(dve, a_hf, u.count(1, 1))
                wait(dve, a_v, u.count(1, -1))
                ve.tensor_copy(tr_hi[:, h, :, :], tr_f[:, h, :, :]).then_inc(a_hi, 1)

            for c in range(NC):
                dve.wait_ge(qkv_step, c + 1)
                last = TT(wqkv_lo[:, c, :], wqkv_raw[:, c, :], wqkv_hi[:, c, :].bitcast(F32), ALU.subtract)
            last.then_inc(qkv_ready, 1)
            split_a(u0)

            dve.wait_ge(d_small, 16 * N_SMALL)
            dve.wait_ge(zero_rows, 1)
            ve.tensor_copy(bqk_t[32:33, :], bqk_raw[32:33, :]).then_inc(bqk_step, 1)
            ve.tensor_copy(bqk_r[0:1, :], bqk_raw[0:1, :])
            dve.wait_ge(bqk_step, 1)
            TT(bqk_r[32:33, :], bqk_raw[32:33, :], bqk_t[32:33, :].bitcast(F32), ALU.subtract).then_inc(bqk_ready, 1)

            n = 2 * NE
            ve.tensor_copy(route_r[:, :, 0:n], route_raw)
            ve.tensor_copy(b2_r[0:n, :], b2_raw[0:n, :])
            ve.tensor_copy(b2_t[32:32 + n, :], b2_raw[32:32 + n, :]).then_inc(small_step, 1)
            dve.wait_ge(small_step, 1)
            TT(route_r[:, :, n:2 * n], route_raw, route_r[:, :, 0:n].bitcast(F32), ALU.subtract)
            TT(b2_r[32:32 + n, :], b2_raw[32:32 + n, :], b2_t[32:32 + n, :].bitcast(F32), ALU.subtract)
            TT(cent_sq[:, :, :], route_raw[:, :, 0:NE], route_raw[:, :, 0:NE], ALU.mult)
            dve.wait_ge(const_ready, 1)
            TT(fold[:, :], ident[0:2 * n, 0:n], ident[0:2 * n, n:2 * n], ALU.add).then_inc(small_ready, 1)

            def mod_rows(b):
                dve.wait_ge(modrow_done, b + 1)
                ga, shift_b = (bank[6][:, k * E:(k + 1) * E] for k in range(2))
                cb, gb = (bank[7][:, k * E:(k + 1) * E] for k in range(2))
                ve.tensor_copy(mod_row[:, b, 1, :], shift_b)
                ve.tensor_scalar(mod_row[:, b, 2, :], cb, 1.0, None, ALU.add)
                both = ((0, ga), (1, gb))
                for i, src in both:
                    last = ve.tensor_scalar(gate_sign[i], src, 0.0, 2.0, ALU.is_ge, ALU.mult)
                last.then_inc(modrow_step, 1)
                dve.wait_ge(modrow_step, MODROW_STEPS * b + 1)
                for i, src in both:
                    last = ve.scalar_tensor_tensor(gate_abs[i], gate_sign[i], -1.0, src, ALU.add, ALU.mult)
                last.then_inc(modrow_step, 1)
                dve.wait_ge(modrow_step, MODROW_STEPS * b + 2)
                for i, src in both:
                    last = ve.tensor_scalar(gate_size[i], gate_abs[i], GATE_MIN, None, ALU.max)
                last.then_inc(modrow_step, 1)
                dve.wait_ge(modrow_step, MODROW_STEPS * b + 3)
                for i, src in both:
                    last = ve.scalar_tensor_tensor(mod_row[:, b, 3 * i, :], gate_sign[i], -1.0, gate_size[i],
                                                   ALU.add, ALU.mult)
                last.then_inc(modrow_step, 1)

            def bias_o(b):
                dve.wait_ge(bo_ready, 1)
                dve.wait_ge(modrow_step, MODROW_STEPS * (b + 1))
                TT(ga_bo[:, b, :], bo_sb, mod_row[:, b, 0, :], ALU.mult).then_inc(ga_bo_ready, 1)

            def feature_map(u, t):
                h = u.h
                wait(dve, a_exp, u.count(2, t + 1))
                if t == 0:
                    wait(dve, a_kv, u.count(1, -1))
                    wait(dve, a_kst, u.count(2, -1))
                ve.scalar_tensor_tensor(q_sb[:, u.tile(t), :], bank[2 + t][:, 0:E], 1.0, e_sb[:, t, 0:E],
                                        ALU.add, ALU.max)
                ve.scalar_tensor_tensor(k_sb[:, h, t, :], bank[2 + t][:, E:2 * E], 1.0, e_sb[:, t, E:2 * E],
                                        ALU.add, ALU.max).then_inc(a_fm, 1)

            def add_kv(u):
                b = u.batch()
                wait(dve, a_kv, u.count(1, 1))
                wait(dve, a_acc, u.count(1, 1))
                acc = kv_acc[:, b, :, :].rearrange("p c n -> p (c n)")
                TT(acc, acc, bank[6 + u.h][:, 0:E], ALU.add).then_inc(a_acc, 1)

            def split_weights(u):
                i = u.count(1, 0)
                if isinstance(i, int):
                    dve.wait_ge(d_w, 48)
                src = w_raw[:, bass.ds(i, 1), :]
                hi = w_hi[:, bass.ds(i, 1), :]
                ve.tensor_copy(hi, src).then_inc(w_hi_done, 1)
                wait(dve, w_hi_done, u.count(1, 1))
                TT(w_lo[:, bass.ds(i, 1), :], src, hi.bitcast(F32), ALU.subtract).then_inc(w_ready, 1)

            def step_a(u):
                if u.plus(-2):
                    add_kv(u.plus(-2))
                if not u.nth(0) and not u.nth(1):
                    split_weights(u)
                if u.plus(1):
                    split_a(u.plus(1))
                feature_map(u, 0)
                feature_map(u, 1)
                for b in range(B):
                    if u.nth(b):
                        split_weights(u)
                        bias_o(b)
                if u.plus(3):
                    stats_a(u.plus(3))

            stats_a(unit(2))
            dve.wait_ge(bo_done, 1)
            ve.tensor_copy(bo_sb, bank[4][:, 0:E]).then_inc(bo_ready, 1)
            mod_rows(0)
            step_a(u0)
            mod_rows(1)
            pipeline(ve, step_a, 1, 2, NU - 4, NU - 3)

            def mask_kv(b, sums):
                dve.wait_ge(f_ksum, b + 1)
                ve.tensor_copy(ksum_row[:, b, :], sums).then_inc(f_ksrow, 1)
                dve.wait_ge(f_ksrow, b + 1)
                dve.wait_ge(a_acc, UPB * (b + 1) + 1)
                wait(dve, f_m, b)
                for c in range(NC):
                    last = ve.scalar_tensor_tensor(kv_b[:, c, :], ksum_row[:, b, c * P:(c + 1) * P],
                                                   bv_sb[:, c:c + 1], kv_acc[:, b, c, :], ALU.mult, ALU.add)
                last.then_inc(f_step, 1)
                dve.wait_ge(f_step, 2 * b + 1)
                for c in range(NC):
                    last = TT(kv_m[:, c, :], kv_b[:, c, :], head_mask[:, :], ALU.mult)
                last.then_inc(f_kvm, 1)

            def split_m(b, product):
                dve.wait_ge(f_m, b + 1)
                for c in range(NC):
                    last = TT(m_f[:, c, :], product[:, c * E:(c + 1) * E], mod_row[:, b, 0, :], ALU.mult)
                last.then_inc(f_m_read, 1)
                dve.wait_ge(f_m_read, b + 1)
                ve.tensor_copy(m_hi[:, b, :, :], m_f[:, :, :]).then_inc(f_step, 1)
                dve.wait_ge(f_step, 2 * b + 2)
                TT(m_lo[:, b, :, :], m_f[:, :, :], m_hi[:, b, :, :].bitcast(F32), ALU.subtract)\
                    .then_inc(f_ready, 1)

            def denominators(u):
                wait(dve, o_prod, u.count(1, 1))
                wait(dve, o_qz, u.count(1, 0))
                ve.tensor_reduce(den[:, :, :].rearrange("p t h -> p (t h)"),
                                 prod[:, :, :].rearrange("p t (h d) -> p (t h) d", d=D),
                                 axis=AXX, op=ALU.add).then_inc(o_den, 1)
                wait(dve, o_den, u.count(2, 1))
                ve.tensor_scalar(den_e[:, :, :], den[:, :, :], DEN_EPS, None, ALU.add).then_inc(o_den, 1)
                wait(dve, o_den, u.count(2, 2))
                ve.reciprocal(z[:, :, :], den_e[:, :, :]).then_inc(o_z, 1)

            def lo_o(u):
                wait(dve, o_hi, u.count(1, 1))
                TT(qz_lo[:, :, :].rearrange("p c n -> p (c n)"), bank[0][:, :],
                   qz_hi[:, :, :].rearrange("p c n -> p (c n)").bitcast(F32), ALU.subtract).then_inc(o_lo, 1)

            def add_attention(u):
                wait(dve, o_y, u.count(2, 2))
                if u.nth(0):
                    dve.wait_ge(a_bo, NU - 4)
                if u.nth(NU - 4):
                    dve.wait_ge(a_bo, NU)
                xt = x_sb[:, bass.ds(u.tile(0), 2), :]
                TT(xt, xt, bank[0][:, :].rearrange("p (t e) -> p t e", t=2), ALU.add).then_inc(o_x1, 1)

            def stats_e(u):
                def x_ready():
                    if u.nth(0):
                        dve.wait_ge(a_rstd, NU)
                    wait_alone(dve, met_v, o_x1, u.count(1, 1))
                stats_of(u, x_ready, e_st, e_stats, e_rstd)

            def modulate_e(u):
                h, b = u.h, u.batch()
                if u.nth(0):
                    dve.wait_ge(a_kv, NU - 1)
                    dve.wait_ge(a_kst, 2 * NU - 1)
                wait(dve, e_rstd, u.count(1, 1))
                wait(dve, e_tp, u.count(1, -1))
                wait(dve, e_sq, u.count(2, -2))
                for t in range(2):
                    ve.scalar_tensor_tensor(xc[:, t, :], x_sb[:, u.tile(t), :], mv[:, h, t, 0:1],
                                            mod_row[:, b, 2, :], ALU.subtract, ALU.mult).then_inc(e_xc, 1)
                for t in range(2):
                    wait(dve, e_xc, u.count(2, t + 1))
                    last = ve.scalar_tensor_tensor(nat[:, h, t, :], xc[:, t, :], rstd[:, h, t:t + 1],
                                                   mod_row[:, b, 1, :], ALU.mult, ALU.add)
                last.then_inc(e_h, 1)

            def clip_norm(u):
                wait(dve, e_sq, u.count(2, 2))
                wait(dve, e_rn, u.count(1, -1))
                ve.tensor_scalar(h_n2c[:, u.h, :], h_n2[:, u.h, :], NORM_EPS2, None, ALU.max).then_inc(e_n2, 1)

            def lo_e(u):
                h = u.h
                wait(dve, e_hi, u.count(1, 1))
                TT(tr_lo[:, h, :, :].rearrange("p c n -> p (c n)"), bank[0][:, :],
                   tr_hi[:, h, :, :].rearrange("p c n -> p (c n)").bitcast(F32), ALU.subtract).then_inc(e_lo, 1)

            def gate(u, p):
                s = p % 2
                wait(dve, e_gelu, u.count(NP, p + 1))
                wait(dve, e_gb, u.count(NP, p + 1))
                wait(dve, *lo_made(u, p - 2))
                TT(hid_g[:, s, :, :].rearrange("p j n -> p (j n)"), hid[:, s, :, :].rearrange("p j n -> p (j n)"),
                   bank[4 + s][:, :], ALU.mult).then_inc(e_mul, 1)

            def lo_hid(u, p):
                s = p % 2
                wait(dve, e_hhi, u.count(NP, p + 1))
                wait(dve, e_f2, u.count(NP, p - 1))
                TT(hid_lo[:, s, :, :], hid_g[:, s, :, :], hid_hi[:, s, :, :].bitcast(F32), ALU.subtract)\
                    .then_inc(e_hlo_v, 1)

            G = 8

            def gates_a(u):
                wait(dve, e_lgT, u.count(1, 1))
                wait(dve, e_rn, u.count(1, 1))
                lg = bank[1][:, 0:4 * NE].rearrange("p (t k) -> p t k", t=2)
                TT(cosw[:, :, :], lg[:, :, 0:NE],
                   cent_rn[:, :].rearrange("p (o e) -> p o e", o=1).to_broadcast([P, 2, NE]), ALU.mult)\
                    .then_inc(e_gstep, 1)
                wait(dve, e_gstep, u.count(G, 1))
                for t in range(2):
                    last = ve.scalar_tensor_tensor(logit[:, t, :], cosw[:, t, :], h_rn[:, u.h, t:t + 1],
                                                   lg[:, t, NE:2 * NE], ALU.mult, ALU.add)
                last.then_inc(e_gstep, 1)
                wait_alone(dve, met_v, e_gstep, u.count(G, 2))
                for t in range(2):
                    last = ve.max(top[:, t, :], logit[:, t, :])
                last.then_inc(e_gstep, 1)
                wait(dve, e_gstep, u.count(G, 3))
                TT(shifted[:, :, :], logit[:, :, :], top[:, :, 0:1].to_broadcast([P, 2, NE]), ALU.subtract)\
                    .then_inc(e_shift, 1)
                TT(chosen[:, :, :], logit[:, :, :], top[:, :, 1:2].to_broadcast([P, 2, NE]), ALU.is_ge)\
                    .then_inc(e_gstep, 1)

            def gates_b(u):
                wait(dve, e_gstep, u.count(G, 4))
                wait(dve, e_gexp, u.count(1, 1))
                TT(g_sel[:, :, :], g_exp[:, :, :], chosen[:, :, :], ALU.mult).then_inc(e_gstep, 1)
                wait(dve, e_gstep, u.count(G, 5))
                ve.tensor_reduce(g_sum[:, :], g_sel[:, :, :], axis=AXX, op=ALU.add).then_inc(e_gstep, 1)
                wait(dve, e_gstep, u.count(G, 6))
                ve.reciprocal(g_rec[:, :], g_sum[:, :]).then_inc(e_gstep, 1)
                wait(dve, e_gstep, u.count(G, 7))
                wait(dve, e_gTp, u.count(1, 0))
                rec = g_rec[:, :].rearrange("p (t o) -> p t o", o=1).to_broadcast([P, 2, NE])
                rec_twice = g_rec[:, :].rearrange("p (t d o) -> p t d o", d=1, o=1).to_broadcast([P, 2, 2, NE])
                sel_twice, f_twice = (m[:, :, :].rearrange("p t (d e) -> p t d e", d=1).to_broadcast([P, 2, 2, NE])
                                      for m in (g_sel, g_f))
                TT(g_f[:, :, :], g_sel[:, :, :], rec, ALU.mult)
                TT(g_hilo[:, :, :, 0:NE], sel_twice, rec_twice, ALU.mult).then_inc(e_gstep, 1)
                wait(dve, e_gstep, u.count(G, 8))
                TT(g_hilo[:, :, :, NE:2 * NE].bitcast(F32), f_twice, g_hilo[:, :, :, 0:NE].bitcast(F32),
                   ALU.subtract)\
                    .then_inc(e_gnat, 1)

            def scale_experts(u):
                b = u.batch()
                wait(dve, e_f2, u.count(NP, NP))
                wait(dve, e_y, u.count(1, 0))
                for t in range(2):
                    last = TT(y_g[:, t, :], bank[6 + t][:, 0:E], mod_row[:, b, 3, :], ALU.mult)
                last.then_inc(e_yg, 1)

            def step_e(u):
                n = u.plus(1)
                if n:
                    clip_norm(n)
                if u:
                    gate(u, 0)
                if u.nth(NU - 1) or u.nth(NU - 2):
                    lo_hid(u, 0)
                if u.plus(3):
                    lo_o(u.plus(3))
                if u.plus(-1):
                    scale_experts(u.plus(-1))
                if u and u.plus(4) and not u.nth(0):
                    denominators(u.plus(4))
                if u:
                    gate(u, 1)
                if u.nth(NU - 1) or u.nth(NU - 2):
                    lo_hid(u, 1)
                if u.nth(0):
                    denominators(u.plus(4))
                if n:
                    gates_a(n)
                if u.nth(-1):
                    mask_kv(1, bank[5][:, 0:E])
                if u.plus(2):
                    modulate_e(u.plus(2))
                if u:
                    gate(u, 2)
                if u.nth(NU - 1) or u.nth(NU - 2):
                    lo_hid(u, 2)
                if u.plus(3):
                    add_attention(u.plus(3))
                if u.nth(-1):
                    denominators(u.plus(4))
                if n:
                    gates_b(n)
                if u.nth(-1):
                    split_m(1, bank[7])
                if u:
                    gate(u, 3)
                if u.nth(NU - 1) or u.nth(NU - 2):
                    lo_hid(u, 3)
                if u.plus(2):
                    lo_e(u.plus(2))
                if u.plus(3):
                    stats_e(u.plus(3))

            mask_kv(0, bank[0][:, 0:E])
            dve.wait_ge(cent_done, 1)
            ve.tensor_scalar(cent_n2[:, :], bank[0][:, E:E + NE], NORM_EPS2, None, ALU.max).then_inc(cent_n2_ready, 1)
            step_a(unit(NU - 3))
            split_m(0, bank[1])
            step_a(unit(NU - 2))
            denominators(u0)
            lo_o(u0)
            denominators(unit(1))
            add_kv(unit(NU - 3))
            split_weights(unit(NU - 1))
            dve.wait_ge(w_ready, NU)
            add_attention(u0)
            feature_map(unit(NU - 1), 0)
            stats_e(u0)
            feature_map(unit(NU - 1), 1)
            lo_o(unit(1))
            add_kv(unit(NU - 2))
            modulate_e(u0)
            add_attention(unit(1))
            denominators(unit(2))
            add_kv(unit(NU - 1))
            lo_e(u0)
            stats_e(unit(1))
            dve.wait_ge(cent_ready, 1)
            step_e(unit(-1))
            pipeline(ve, step_e, 0, 2, NU - 4)
            dve.wait_ge(e_y, NU - 1)
            for t in range(2):
                dve.wait_ge(last_f2, t + 1)
                TT(y_g[:, t, :], bank[6 + t][:, 0:E], mod_row[:, B - 1, 3, :], ALU.mult).then_inc(last_scaled, 1)
                dve.wait_ge(last_scaled, t + 1)
                xt = x_sb[:, NT - 2 + t, :]
                TT(xt, xt, y_g[:, t, :], ALU.add).then_inc(last_y, 1)


def kernel(**inputs):
    import numpy as np
    import concourse.bacc as bacc
    from concourse.bass_utils import run_bass_kernel_spmd

    a = {k.replace("L0_", ""): np.asarray(v) for k, v in inputs.items()}
    B, S, E = a["attn_x"].shape
    route = np.concatenate([a["ffn_centroids"].T, a["ffn_w_route"].T], axis=1)
    given = {
        "x": a["attn_x"].reshape(B * S, E),
        "wqkvT": np.concatenate([a["attn_Wq"].T, a["attn_Wk"].T, a["attn_Wv"].T], axis=1),
        "rows": np.concatenate([a["attn_bq"], a["attn_bk"], a["attn_bo"]]).reshape(1, 3 * E),
        "cols": np.concatenate([route[:P], route[P:], a["attn_bv"].reshape(2, P).T, a["ffn_b1"].T], axis=1),
        "woT": a["attn_Wo"].T,
        "w1": a["ffn_w1"],
        "w2": a["ffn_w2"],
        "b2": np.concatenate([a["ffn_b2"], a["ffn_b2"]]),
        "cT": a["c"].T,
        "wmod": a["wmod"],
    }
    nc = bacc.Bacc("TRN2", target_bir_lowering=False, num_devices=1)
    arrays, args = {}, []
    for name, value in given.items():
        value = np.ascontiguousarray(value)
        arrays[f"in_{name}"] = value
        args.append(nc.dram_tensor(f"in_{name}", value.shape, mybir.dt.from_np(value.dtype), kind="ExternalInput").ap())
    out = nc.dram_tensor("out_0", (B * S, E), F32, kind="ExternalOutput").ap()
    adaln_block(nc, *args, out)
    got = run_bass_kernel_spmd(nc, [arrays], core_ids=[0])
    return got.results[0]["out_0"].reshape(B, S, E)
```
